# Optimizing a Trainium2 kernel written in Bass

```python
import numpy as np
import jax
import jax.numpy as jnp

def _softmax(x, axis=-1):
    return jax.nn.softmax(x, axis=axis)

def _gelu(x):
    return jax.nn.gelu(x, approximate=True)

def _silu(x):
    return jax.nn.silu(x)

def _sigmoid(x):
    return jax.nn.sigmoid(x)

def _layernorm(x, axis=-1, eps=1e-05):
    m = jnp.mean(x, axis=axis, keepdims=True)
    v = jnp.var(x, axis=axis, keepdims=True)
    return (x - m) / jnp.sqrt(v + eps)

def _scatter_add(tgt, idx, src, axis=0):
    return tgt.at[idx].add(src)

def _segment_sum(src, seg, n):
    return jax.ops.segment_sum(src, seg, n)
kernel_name = 'mk_gnn_resnorm_d2_gnn_r8_903ce2'

def setup_inputs(seed: int=0):
    np.random.seed(seed)
    _w = jnp.asarray

    def _rec_inputs():
        import jax
        import jax.numpy as jnp
        _gk = jax.random.key(seed)
        x = -0.000202 + 1 * jax.random.normal(jax.random.fold_in(_gk, 1), (6250, 128), jnp.float32)
        _s = jax.random.randint(jax.random.fold_in(_gk, 2), (50000,), 0, 6250, jnp.int32)
        _d = jax.random.randint(jax.random.fold_in(_gk, 3), (50000,), 0, 6250, jnp.int32)
        _loop = jnp.arange(6250, dtype=jnp.int32)
        src = jnp.concatenate([_s, _d, _loop])
        dst = jnp.concatenate([_d, _s, _loop])
        _o = jnp.argsort(dst, stable=True)
        src = src[_o]
        dst = dst[_o]
        edge_attr_4 = -0.000107899 + 1.00008 * jax.random.normal(jax.random.fold_in(_gk, 11), (106250, 4), jnp.float32)
        edge_attr_8 = jax.random.uniform(jax.random.fold_in(_gk, 12), (106250, 8), jnp.float32, 0.0, 1)
        return (x, src, dst, edge_attr_4, edge_attr_8)
    x, src, dst, edge_attr_4, edge_attr_8 = _rec_inputs()

    def _L0_gnn_setup():
        import jax, jax.numpy as jnp
        import numpy as np
        N = 6250
        DEG = 16
        DIM = 128
        H = 128

        def _lstm_last(seq, w_ih, w_hh, b):
            n = seq.shape[0]
            h_dim = w_hh.shape[1]
            h0 = jnp.zeros((n, h_dim), seq.dtype)

            def step(carry, x_t):
                h, c = carry
                gates = x_t @ w_ih.T + h @ w_hh.T + b
                i, f, g, o = jnp.split(gates, 4, axis=-1)
                c = jax.nn.sigmoid(f) * c + jax.nn.sigmoid(i) * jnp.tanh(g)
                h = jax.nn.sigmoid(o) * jnp.tanh(c)
                return ((h, c), None)
            (h, _), _ = jax.lax.scan(step, (h0, h0), jnp.swapaxes(seq, 0, 1))
            return h
        key = jax.random.key(seed)
        ks = jax.random.split(key, 8)
        x = jax.random.normal(ks[0], (N, DIM), dtype=jnp.float32)
        row = jnp.repeat(jnp.arange(N), DEG)
        col = jax.random.randint(ks[1], (N * DEG,), 0, N)
        edge_index = jnp.stack([row, col]).astype(jnp.int32)
        s = 1.0 / np.sqrt(H)
        w_ih = jax.random.uniform(ks[2], (4 * H, DIM), jnp.float32, -s, s)
        w_hh = jax.random.uniform(ks[3], (4 * H, H), jnp.float32, -s, s)
        b_ih = jax.random.uniform(ks[4], (4 * H,), jnp.float32, -s, s)
        b_hh = jax.random.uniform(ks[5], (4 * H,), jnp.float32, -s, s)
        w_lin = jax.random.uniform(ks[6], (H, H), jnp.float32, -s, s)
        b_lin = jax.random.uniform(ks[7], (H,), jnp.float32, -s, s)
        return {'x': x, 'edge_index': edge_index, 'w_ih': w_ih, 'w_hh': w_hh, 'b_ih': b_ih, 'b_hh': b_hh, 'w_lin': w_lin, 'b_lin': b_lin}
    _L0_gnn_all = _L0_gnn_setup()
    _L0_gnn_in = {k: v for k, v in _L0_gnn_all.items() if k in ('w_ih', 'w_hh', 'b_ih', 'b_hh', 'w_lin', 'b_lin')}
    del _L0_gnn_all

    def _L1_gnn_setup():
        import jax, jax.numpy as jnp
        import numpy as np
        MUL = 32
        N_NODES = 6250
        N_EDGES = 100000
        R3 = np.sqrt(3.0).astype(np.float32)
        key = jax.random.key(seed)
        ks = jax.random.split(key, 12)
        inp = {}
        inp['node_feats'] = jax.random.normal(ks[0], (N_NODES, 4 * MUL), dtype=jnp.float32)
        inp['edge_attrs'] = jax.random.normal(ks[1], (N_EDGES, 4), dtype=jnp.float32)
        inp['edge_feats'] = jax.random.uniform(ks[2], (N_EDGES, 8), dtype=jnp.float32)
        inp['edge_index'] = jax.random.randint(ks[3], (2, N_EDGES), 0, N_NODES)
        inp['W_up_s'] = jax.random.normal(ks[4], (MUL, MUL), dtype=jnp.float32)
        inp['W_up_v'] = jax.random.normal(ks[5], (MUL, MUL), dtype=jnp.float32)
        inp['A1'] = jax.random.normal(ks[6], (8, 64), dtype=jnp.float32) / np.sqrt(8.0)
        inp['b1'] = jnp.zeros((64,), dtype=jnp.float32)
        inp['A2'] = jax.random.normal(ks[7], (64, 64), dtype=jnp.float32) / np.sqrt(64.0)
        inp['b2'] = jnp.zeros((64,), dtype=jnp.float32)
        inp['A3'] = jax.random.normal(ks[8], (64, 4 * MUL), dtype=jnp.float32) * (10.0 * np.sqrt(6.0 / (64 + 4 * MUL)))
        inp['W_out_s'] = jax.random.normal(ks[9], (2 * MUL, MUL), dtype=jnp.float32)
        inp['W_out_v'] = jax.random.normal(ks[10], (2 * MUL, MUL), dtype=jnp.float32)
        return inp
    _L1_gnn_all = _L1_gnn_setup()
    _L1_gnn_in = {k: v for k, v in _L1_gnn_all.items() if k in ('W_up_s', 'W_up_v', 'A1', 'b1', 'A2', 'b2', 'A3', 'W_out_s', 'W_out_v')}
    del _L1_gnn_all
    return {'x': x, 'src': src, 'dst': dst, 'edge_attr_4': edge_attr_4, 'edge_attr_8': edge_attr_8, 'L0_gnn_w_ih': _L0_gnn_in['w_ih'], 'L0_gnn_w_hh': _L0_gnn_in['w_hh'], 'L0_gnn_b_ih': _L0_gnn_in['b_ih'], 'L0_gnn_b_hh': _L0_gnn_in['b_hh'], 'L0_gnn_w_lin': _L0_gnn_in['w_lin'], 'L0_gnn_b_lin': _L0_gnn_in['b_lin'], 'L1_gnn_W_up_s': _L1_gnn_in['W_up_s'], 'L1_gnn_W_up_v': _L1_gnn_in['W_up_v'], 'L1_gnn_A1': _L1_gnn_in['A1'], 'L1_gnn_b1': _L1_gnn_in['b1'], 'L1_gnn_A2': _L1_gnn_in['A2'], 'L1_gnn_b2': _L1_gnn_in['b2'], 'L1_gnn_A3': _L1_gnn_in['A3'], 'L1_gnn_W_out_s': _L1_gnn_in['W_out_s'], 'L1_gnn_W_out_v': _L1_gnn_in['W_out_v']}

def reference(x, src, dst, edge_attr_4, edge_attr_8, L0_gnn_w_ih, L0_gnn_w_hh, L0_gnn_b_ih, L0_gnn_b_hh, L0_gnn_w_lin, L0_gnn_b_lin, L1_gnn_W_up_s, L1_gnn_W_up_v, L1_gnn_A1, L1_gnn_b1, L1_gnn_A2, L1_gnn_b2, L1_gnn_A3, L1_gnn_W_out_s, L1_gnn_W_out_v):
    import jax
    import jax.numpy as jnp

    def _L0_gnn_ref(x, edge_index, w_ih, w_hh, b_ih, b_hh, w_lin, b_lin):
        import jax, jax.numpy as jnp
        import numpy as np
        N = 6250
        DEG = 16
        DIM = 128
        H = 128

        def _lstm_last(seq, w_ih, w_hh, b):
            n = seq.shape[0]
            h_dim = w_hh.shape[1]
            h0 = jnp.zeros((n, h_dim), seq.dtype)

            def step(carry, x_t):
                h, c = carry
                gates = x_t @ w_ih.T + h @ w_hh.T + b
                i, f, g, o = jnp.split(gates, 4, axis=-1)
                c = jax.nn.sigmoid(f) * c + jax.nn.sigmoid(i) * jnp.tanh(g)
                h = jax.nn.sigmoid(o) * jnp.tanh(c)
                return ((h, c), None)
            (h, _), _ = jax.lax.scan(step, (h0, h0), jnp.swapaxes(seq, 0, 1))
            return h
        n, d = x.shape
        deg = edge_index.shape[1] // n
        col = edge_index[1]
        seq = x[col].reshape(n, deg, d)
        h_last = _lstm_last(seq, w_ih, w_hh, b_ih + b_hh)
        return h_last @ w_lin.T + b_lin

    def _L1_gnn_ref(node_feats, edge_attrs, edge_feats, W_up_s, W_up_v, A1, b1, A2, b2, A3, W_out_s, W_out_v, edge_index):
        import jax, jax.numpy as jnp
        import numpy as np
        MUL = 32
        N_NODES = 6250
        N_EDGES = 100000
        R3 = np.sqrt(3.0).astype(np.float32)
        num_nodes = node_feats.shape[0]
        sender, receiver = (edge_index[0], edge_index[1])
        s = node_feats[:, :MUL]
        v = node_feats[:, MUL:].reshape(num_nodes, MUL, 3)
        inv = 1.0 / np.sqrt(MUL).astype(np.float32)
        s = s @ W_up_s * inv
        v = jnp.einsum('nui,uw->nwi', v, W_up_v) * inv
        h = jax.nn.silu(edge_feats @ A1 + b1)
        h = jax.nn.silu(h @ A2 + b2)
        tpw = h @ A3
        w0, w1, w2, w3 = jnp.split(tpw, 4, axis=1)
        ss = s[sender]
        vs = v[sender]
        y_s = edge_attrs[:, :1]
        y_v = edge_attrs[:, 1:4]
        out_s0 = ss * y_s * w0
        out_s3 = jnp.einsum('eui,ei->eu', vs, y_v) / R3 * w3
        out_v1 = ss[:, :, None] * y_v[:, None, :] * w1[:, :, None]
        out_v2 = vs * y_s[:, :, None] * w2[:, :, None]
        E = ss.shape[0]
        mji = jnp.concatenate([out_s0, out_s3, out_v1.reshape(E, 3 * MUL), out_v2.reshape(E, 3 * MUL)], axis=1)
        message = jax.ops.segment_sum(mji, receiver, num_segments=num_nodes) / 10.0
        ms = message[:, :2 * MUL]
        mv = message[:, 2 * MUL:].reshape(num_nodes, 2 * MUL, 3)
        inv2 = 1.0 / np.sqrt(2 * MUL).astype(np.float32)
        out_s = ms @ W_out_s * inv2
        out_v = jnp.einsum('nui,uw->nwi', mv, W_out_v) * inv2
        return jnp.concatenate([out_s, out_v.reshape(num_nodes, 3 * MUL)], axis=1)
    edge_index = jnp.stack([src, dst])
    x = _layernorm(x + _L0_gnn_ref(x, edge_index, L0_gnn_w_ih, L0_gnn_w_hh, L0_gnn_b_ih, L0_gnn_b_hh, L0_gnn_w_lin, L0_gnn_b_lin), axis=-1)
    x = _layernorm(x + _L1_gnn_ref(x, edge_attr_4, edge_attr_8, L1_gnn_W_up_s, L1_gnn_W_up_v, L1_gnn_A1, L1_gnn_b1, L1_gnn_A2, L1_gnn_b2, L1_gnn_A3, L1_gnn_W_out_s, L1_gnn_W_out_v, edge_index), axis=-1)
    return x

_drawn_inputs = setup_inputs


def setup_inputs(seed=0):
    import zlib

    import numpy as np

    out = dict(_drawn_inputs(seed))
    spreads = {'L1_gnn_b1': (0.0, 0.1), 'L1_gnn_b2': (0.0, 0.1)}
    factors = {'L0_gnn_b_ih': 4.056, 'L0_gnn_b_hh': 4.669}
    for name, (base, spread) in spreads.items():
        noise = np.random.default_rng([zlib.crc32(name.encode()), seed]).standard_normal(out[name].shape)
        drawn = base * np.exp(spread * noise) if base else spread * noise
        out[name] = jnp.asarray(drawn.astype(out[name].dtype))
    for name, factor in factors.items():
        out[name] = (out[name] * factor).astype(out[name].dtype)
    return out
```

```python
from contextlib import ExitStack

import numpy as np

import concourse.bass as bass
from concourse import mybir

F32 = mybir.dt.float32
I32 = mybir.dt.int32
BF16 = mybir.dt.bfloat16
ALU = mybir.AluOpType
ACT = mybir.ActivationFunctionType

P = 128
NODES, DIM, HID = 6250, 128, 128
EDGES = 106250
STEPS = EDGES // NODES
MUL = 32
NODE_TILES = -(-NODES // P)
NODE_COLS = NODE_TILES * P
LAST_ROWS = NODES - (NODE_TILES - 1) * P

CHUNK = 512
CHUNKS = [(c, min(CHUNK, NODE_COLS - c)) for c in range(0, NODE_COLS, CHUNK)]
NCH = len(CHUNKS)
WORK = [(t, c) for t in range(STEPS) for c in range(NCH)]
GATES = (0, 2, 1, 3)

GROUP = 8
HALF = GROUP // 2
SUPER = 64
EDGE_TILES = -(-(-(-EDGES // P)) // SUPER) * SUPER
NGROUP = EDGE_TILES // GROUP
WIN = 80
ROUNDS = -(-NODES // WIN)
TURN = ROUNDS * WIN
FAR = 1 << 24


PAIR = (4, 6, 7)


def window_bases():
    centre = (np.arange(EDGE_TILES) + 0.5) * P * NODES / EDGES
    base = np.clip(np.rint(centre - WIN / 2), 0, None).astype(int)
    width = max(base[g * GROUP + GROUP - 1] - base[g * GROUP] for g in range(NGROUP)) + WIN
    width += width % 2
    base = np.minimum(base, TURN - width)
    return base, width


BASE, GWIDTH = window_bases()


def build(nc, t):
    ctx = ExitStack()
    with ctx:
        def sb(name, shape, dt=F32, scope=ctx):
            return scope.enter_context(nc.sbuf_tensor(name, shape, dt))

        def ps(name, shape, dt=F32, scope=ctx):
            return scope.enter_context(nc.psum_tensor(name, shape, dt))

        def sem(name):
            return ctx.enter_context(nc.semaphore(name))

        x1 = sb("x1", [P, NODE_TILES, DIM])
        dst = sb("dst", [P, EDGE_TILES])
        rel = sb("rel", [P, EDGE_TILES])
        base_row = sb("base_row", [P, EDGE_TILES])
        src_index = sb("src_index", [P, EDGE_TILES], I32)
        attr = sb("attr", [P, 4, EDGE_TILES])
        node_iota = sb("node_iota", [P, WIN])
        ones = sb("ones", [P, P])
        ident = sb("ident", [P, P])
        eps = sb("eps", [P, 1])
        w_up = sb("w_up", [P, P])
        a1 = sb("a1", [P, GROUP * P])
        a2 = sb("a2", [P, P])
        a3 = sb("a3", [P, P])
        b12 = sb("b12", [P, 2])
        w_out = sb("w_out", [P, 3 * P])
        w_lin = sb("w_lin", [P, P])
        b_lin = sb("b_lin", [1, P])
        rounds_word = sb("rounds_word", [1, 1], I32)
        zeros = sb("zeros", [P, 3 * GWIDTH], BF16)
        stats = sb("stats", [P, NODE_TILES, 6])
        moments = sb("moments", [P, NODE_TILES, 2])
        rstd = sb("rstd", [P, NODE_TILES])

        banks = [ps(f"bank{i}", [P, 512]) for i in range(8)]

        s_const = sem("s_const")
        s_wait = [sem(f"s_gather{i}") for i in range(4)]

        with ExitStack() as scope:
            w_ih = sb("w_ih", [P, 4 * HID], scope=scope)
            w_hh = sb("w_hh", [P, 4 * HID], scope=scope)
            bias2 = sb("bias2", [P, 8], scope=scope)
            bias = sb("bias", [P, 4], scope=scope)
            seq_index = sb("seq_index", [P, NODE_TILES * STEPS], I32, scope=scope)
            dst_int = sb("dst_int", [P, EDGE_TILES], I32, scope=scope)
            inside = sb("inside", [P, EDGE_TILES], scope=scope)
            inside2 = sb("inside2", [P, EDGE_TILES], scope=scope)
            count = sb("count", [P, 1], scope=scope)
            missed = sb("missed", [1, 1], scope=scope)
            hidden = sb("hidden", [P, NODE_COLS], scope=scope)
            cell = sb("cell", [P, NODE_COLS], scope=scope)
            rows = sb("rows", [P, 4, 4, DIM], scope=scope)
            xt = sb("xt", [P, 2, CHUNK], scope=scope)
            act = sb("act", [P, 2, 4, CHUNK], scope=scope)
            tanh_c = sb("tanh_c", [P, 2, CHUNK], scope=scope)
            prod_ig = sb("prod_ig", [P, CHUNK], scope=scope)
            prod_fc = sb("prod_fc", [P, CHUNK], scope=scope)

            s_idx, s_wts, s_rest = sem("s_idx"), sem("s_wts"), sem("s_rest")
            s_turned, s_xt = sem("s_turned"), sem("s_xt")
            s_gate, s_act = sem("s_gate"), sem("s_act")
            s_cell, s_tanh, s_hidden = sem("s_cell"), sem("s_tanh"), sem("s_hidden")
            s_ig, s_fc, s_bias, s_prep = sem("s_ig"), sem("s_fc"), sem("s_bias"), sem("s_prep")
            s_count = sem("s_count")
            s_set = sem("s_set")

            turned_bank = [banks[6], banks[7]]
            gate_bank = banks[:6]

            with nc.Block() as block:
                @block.sync
                def _(sp):
                    sp.dma_start(seq_index[:], t["seq_index"]).then_inc(s_idx, 16)
                    for tile, name in ((ident, "ident"), (w_ih, "w_ih"), (w_hh, "w_hh"), (bias2, "bias2")):
                        sp.dma_start(tile[:], t[name]).then_inc(s_wts, 16)
                    sp.dma_start(dst_int[:], t["dst"]).then_inc(s_const, 16)
                    sp.dma_start(base_row[:], t["base_row"]).then_inc(s_const, 16)
                    sp.dma_start(node_iota[:], t["node_iota"]).then_inc(s_rest, 16)
                    sp.dma_start(x1[:].rearrange("p a d -> p (a d)"), t["x_nodes"]).then_inc(s_rest, 16)
                    sp.dma_start(src_index[:], t["src"]).then_inc(s_rest, 16)
                    sp.dma_start(attr[:].rearrange("p k e -> p (k e)"), t["attr4"]).then_inc(s_rest, 16)
                    for tile, name in ((w_up, "w_up"), (a1, "a1"), (a2, "a2"), (a3, "a3"), (b12, "b12"),
                                       (w_out, "w_out"), (w_lin, "w_lin"), (b_lin, "b_lin")):
                        sp.dma_start(tile[:], t[name]).then_inc(s_rest, 16)
                    sp.wait_ge(s_rest, 16 * 12)

                @block.gpsimd
                def _(pool):
                    pool.memset(ones[:], 1.0).then_inc(s_set, 1)
                    pool.memset(eps[:], 1e-5).then_inc(s_set, 1)
                    pool.memset(zeros[:], 0.0).then_inc(s_set, 1)
                    pool.wait_ge(s_idx, 16)
                    landed = [0] * 4
                    for k, (step, c) in enumerate(WORK):
                        if k >= 4:
                            pool.wait_ge(s_turned, k - 3)
                        c0, width = CHUNKS[c]
                        for j in range(width // P):
                            col = (c0 // P + j) * STEPS + step
                            pool.indirect_dma_start(
                                out=rows[:, k % 4, j, :], out_offset=None, in_=t["x"],
                                in_offset=bass.IndirectOffsetOnAxis(ap=seq_index[:, col:col + 1], axis=0),
                            ).then_inc(s_wait[k % 4], 16)

                @block.tensor
                def _(pe):
                    landed = [0] * 4

                    def turn(k):
                        c0, width = CHUNKS[WORK[k][1]]
                        landed[k % 4] += 16 * (width // P)
                        pe.wait_ge(s_wait[k % 4], landed[k % 4])
                        if k >= 2:
                            pe.wait_ge(s_xt, k - 1)
                        for j in range(width // P):
                            last = pe.transpose(turned_bank[k % 2][:, j * P:(j + 1) * P],
                                                rows[:, k % 4, j, :], ident[:])
                        last.then_inc(s_turned, 1)

                    pe.wait_ge(s_wts, 64)
                    turn(0)
                    for k, (step, c) in enumerate(WORK):
                        if k + 1 < len(WORK):
                            turn(k + 1)
                        c0, width = CHUNKS[c]
                        pe.wait_ge(s_xt, k + 1)
                        for q, gate in enumerate(GATES):
                            n = 4 * k + q
                            if n >= 6:
                                pe.wait_ge(s_act, n - 5)
                            out = gate_bank[n % 6][:, 0:width]
                            last = pe.matmul(out, w_ih[:, gate * HID:(gate + 1) * HID], xt[:, k % 2, 0:width],
                                             start=True, stop=(step == 0))
                            if step:
                                if q == 0:
                                    pe.wait_ge(s_hidden, k - NCH + 1)
                                last = pe.matmul(out, w_hh[:, gate * HID:(gate + 1) * HID],
                                                 hidden[:, c0:c0 + width], start=False, stop=True)
                            last.then_inc(s_gate, 1)
                    pe.wait_ge(s_prep, 5)
                    pe.wait_ge(s_set, 1)
                    pe.matmul(turned_bank[0][0:1, 0:1], count[:], ones[:, 0:1], start=True, stop=True).then_inc(s_count, 1)

                @block.scalar
                def _(act_e):
                    def tanh_cell(k):
                        c0, width = CHUNKS[WORK[k][1]]
                        act_e.wait_ge(s_cell, k + 1)
                        if k >= 2:
                            act_e.wait_ge(s_hidden, k - 1)
                        act_e.activation(tanh_c[:, k % 2, 0:width], cell[:, c0:c0 + width],
                                         ACT.Tanh).then_inc(s_tanh, 1)

                    act_e.wait_ge(s_bias, 1)
                    for k, (step, c) in enumerate(WORK):
                        width = CHUNKS[c][1]
                        for q, gate in enumerate(GATES):
                            n = 4 * k + q
                            if q == 0 and k >= 2:
                                act_e.wait_ge(s_hidden, k - 1)
                            act_e.wait_ge(s_gate, n + 1)
                            act_e.activation(act[:, k % 2, gate, 0:width], gate_bank[n % 6][:, 0:width],
                                             ACT.Tanh if gate == 2 else ACT.Sigmoid,
                                             bias=bias[:, gate:gate + 1]).then_inc(s_act, 1)
                        if k:
                            tanh_cell(k - 1)
                    tanh_cell(len(WORK) - 1)

                @block.vector
                def _(dve):
                    def copy_turned(k):
                        width = CHUNKS[WORK[k][1]][1]
                        dve.wait_ge(s_turned, k + 1)
                        if k >= 2:
                            dve.wait_ge(s_gate, 4 * (k - 1))
                        dve.tensor_copy(xt[:, k % 2, 0:width], turned_bank[k % 2][:, 0:width]).then_inc(s_xt, 1)

                    def new_hidden(k):
                        c0, width = CHUNKS[WORK[k][1]]
                        dve.wait_ge(s_tanh, k + 1)
                        dve.tensor_tensor(hidden[:, c0:c0 + width], act[:, k % 2, 3, 0:width],
                                          tanh_c[:, k % 2, 0:width], ALU.mult).then_inc(s_hidden, 1)

                    dve.wait_ge(s_wts, 64)
                    dve.tensor_tensor(bias[:], bias2[:, 0:4], bias2[:, 4:8], ALU.add).then_inc(s_bias, 1)
                    copy_turned(0)
                    for k, (step, c) in enumerate(WORK):
                        c0, width = CHUNKS[c]
                        if k + 1 < len(WORK):
                            copy_turned(k + 1)
                        if k:
                            new_hidden(k - 1)
                        here = cell[:, c0:c0 + width]
                        gates = act[:, k % 2, :, 0:width]
                        if step == 0:
                            dve.wait_ge(s_act, 4 * k + 2)
                            dve.tensor_tensor(here, gates[:, 0], gates[:, 2], ALU.mult).then_inc(s_cell, 1)
                            dve.wait_ge(s_act, 4 * k + 4)
                            continue
                        n = k - NCH + 1
                        dve.wait_ge(s_act, 4 * k + 2)
                        dve.wait_ge(s_cell, k)
                        dve.tensor_tensor(prod_ig[:, 0:width], gates[:, 0], gates[:, 2], ALU.mult).then_inc(s_ig, 1)
                        dve.wait_ge(s_act, 4 * k + 3)
                        dve.tensor_tensor(prod_fc[:, 0:width], gates[:, 1], here, ALU.mult).then_inc(s_fc, 1)
                        dve.wait_ge(s_ig, n)
                        dve.wait_ge(s_fc, n)
                        dve.tensor_tensor(here, prod_ig[:, 0:width], prod_fc[:, 0:width], ALU.add).then_inc(s_cell, 1)
                        dve.wait_ge(s_act, 4 * k + 4)
                    new_hidden(len(WORK) - 1)
                    dve.wait_ge(s_const, 32)
                    dve.tensor_copy(dst[:], dst_int[:]).then_inc(s_prep, 1)
                    dve.wait_ge(s_prep, 1)
                    dve.tensor_tensor(rel[:], dst[:], base_row[:], ALU.subtract).then_inc(s_prep, 1)
                    dve.wait_ge(s_prep, 2)
                    dve.tensor_scalar(inside[:], rel[:], 0.0, None, ALU.is_ge).then_inc(s_prep, 1)
                    dve.wait_ge(s_prep, 3)
                    dve.scalar_tensor_tensor(inside2[:], rel[:], float(WIN), inside[:], ALU.is_lt,
                                             ALU.mult).then_inc(s_prep, 1)
                    dve.wait_ge(s_prep, 4)
                    dve.tensor_reduce(count[:], inside2[:], mybir.AxisListType.X, ALU.add).then_inc(s_prep, 1)
                    dve.wait_ge(s_count, 1)
                    dve.tensor_scalar(missed[:], turned_bank[0][0:1, 0:1], float(EDGES), float(ROUNDS - 1),
                                      ALU.is_lt, ALU.mult).then_inc(s_prep, 1)
                    dve.wait_ge(s_prep, 6)
                    dve.tensor_scalar(rounds_word[:], missed[:], 1.0, None, ALU.add).then_inc(s_prep, 1)
                    dve.wait_ge(s_prep, 7)

            x1t = sb("x1t", [P, 2, P], scope=scope)
            up = sb("up", [P, 4, P], scope=scope)
            s_po, s_sum, s_mom, s_sqrt, s_rstd, s_norm = (sem(n) for n in (
                "s_po", "s_sum", "s_mom", "s_sqrt", "s_rstd", "s_norm"))
            s_st, s_x1t, s_x1c, s_upp, s_up = (sem(n) for n in ("s_st", "s_x1t", "s_x1c", "s_upp", "s_up"))
            s_table = [sem(f"s_table{i}") for i in range(4)]
            with nc.Block() as block:
                @block.tensor
                def _(pe):
                    for n in range(NODE_TILES):
                        if n >= 4:
                            pe.wait_ge(s_sum, n - 3)
                        out = banks[n % 4][:, 0:P]
                        pe.matmul(out, hidden[:, n * P:(n + 1) * P], w_lin[:], start=True, stop=False)
                        pe.matmul(out, ones[0:1, :], b_lin[:], start=False, stop=True).then_inc(s_po, 1)
                    for n in range(NODE_TILES):
                        pe.wait_ge(s_norm, n + 1)
                        if n >= 2:
                            pe.wait_ge(s_x1c, n - 1)
                        pe.transpose(banks[4 + n % 2][:, 0:P], x1[:, n, :], ident[:]).then_inc(s_x1t, 1)
                        pe.wait_ge(s_x1c, n + 1)
                        if n >= 2:
                            pe.wait_ge(s_up, n - 1)
                        pe.matmul(banks[6 + n % 2][:, 0:P], x1t[:, n % 2, :], w_up[:],
                                  start=True, stop=True).then_inc(s_upp, 1)

                @block.vector
                def _(dve):
                    for n in range(NODE_TILES):
                        dve.wait_ge(s_po, n + 1)
                        dve.tensor_tensor(x1[:, n, :], banks[n % 4][:, 0:P], x1[:, n, :], ALU.add).then_inc(s_sum, 1)
                        dve.wait_ge(s_sum, n + 1)
                        dve.bn_stats(stats[:, n, :], x1[:, n, :]).then_inc(s_st, 1)
                        dve.wait_ge(s_st, n + 1)
                        dve.bn_aggr(moments[:, n, :], stats[:, n, :]).then_inc(s_mom, 1)
                    dve.wait_ge(s_sqrt, 1)
                    dve.reciprocal(rstd[:], rstd[:]).then_inc(s_rstd, 1)
                    dve.wait_ge(s_rstd, 1)
                    for n in range(NODE_TILES):
                        dve.tensor_scalar(x1[:, n, :], x1[:, n, :], moments[:, n, 0:1], rstd[:, n:n + 1],
                                          ALU.subtract, ALU.mult).then_inc(s_norm, 1)

                def projected(act_e, n):
                    act_e.wait_ge(s_upp, n + 1)
                    if n >= 4:
                        act_e.wait_ge(s_table[n % 4], 16 * (n // 4))
                    act_e.activation(up[:, n % 4, :], banks[6 + n % 2][:, 0:P], ACT.Copy,
                                     scale=float(1 / np.sqrt(np.float32(MUL)))).then_inc(s_up, 1)

                @block.scalar
                def _(act_e):
                    act_e.wait_ge(s_mom, NODE_TILES)
                    act_e.activation(rstd[:], moments[:, :, 1], ACT.Sqrt, bias=eps[:]).then_inc(s_sqrt, 1)
                    for n in range(NODE_TILES):
                        act_e.wait_ge(s_x1t, n + 1)
                        if n >= 2:
                            act_e.wait_ge(s_upp, n - 1)
                        act_e.activation(x1t[:, n % 2, :], banks[4 + n % 2][:, 0:P], ACT.Copy).then_inc(s_x1c, 1)
                        if n:
                            projected(act_e, n - 1)
                    projected(act_e, NODE_TILES - 1)

                @block.sync
                def _(sp):
                    for n in range(NODE_TILES):
                        sp.wait_ge(s_up, n + 1)
                        sp.dma_start(t["table"][n * P:(n + 1) * P, :], up[:, n % 4, :]).then_inc(s_table[n % 4], 16)
                    for i in range(4):
                        sp.wait_ge(s_table[i], 16 * len(range(i, NODE_TILES, 4)))

        acc = sb("acc", [P, 3, TURN])
        feats = sb("feats", [P, 2, 512])
        h1 = sb("h1", [P, 2, 512])
        h2 = sb("h2", [P, 2, 512])
        sender = sb("sender", [P, 4, HALF, P])
        msg = sb("msg", [P, 2, HALF, 9, MUL])
        select = sb("select", [P, 2, HALF, 4, WIN])
        wrap = sb("wrap", [P, EDGE_TILES])

        e_rel, e_zero, e_turn = sem("e_rel"), sem("e_zero"), sem("e_turn")
        e_feats = [sem("e_feats0"), sem("e_feats1")]
        e_gather = [sem(f"e_gather{i}") for i in range(4)]
        e_p1, e_h1, e_p2, e_h2, e_w = (sem(n) for n in ("e_p1", "e_h1", "e_p2", "e_h2", "e_w"))
        e_sel, e_msg, e_half, e_group, e_acc = (sem(n) for n in ("e_sel", "e_msg", "e_half", "e_group", "e_acc"))
        e_sems = [e_rel, e_zero, e_turn, *e_feats, *e_gather, e_p1, e_h1, e_p2, e_h2, e_w,
                  e_sel, e_msg, e_half, e_group, e_acc]
        p1_bank, p2_bank = banks[0], banks[1]
        weight_bank, acc_bank = banks[2:5], banks[5:7]
        NHALF = 2 * NGROUP

        with nc.Block() as block:
            @block.gpsimd
            def _(pool):
                pool.memset(acc[:].rearrange("p a b -> p (a b)"), 0.0).then_inc(e_zero, 1)
                pool.wait_ge(e_zero, 1)
                pool.sem_clear(e_zero)
        rounds = nc.values_load(rounds_word[0:1, 0:1], min_val=1, max_val=ROUNDS)

        with nc.Fori(0, rounds):
            with nc.Block() as block:
                @block.sync
                def _(sp):
                    for s in range(EDGE_TILES // SUPER):
                        if s >= 2:
                            sp.wait_ge(e_p1, GROUP * (s - 1))
                        sp.dma_start(feats[:, s % 2, :], t["attr8"][s]).then_inc(e_feats[s % 2], 16)

                @block.gpsimd
                def _(pool):
                    for hg in range(NHALF):
                        if hg >= 4:
                            pool.wait_ge(e_msg, hg - 3)
                        for j in range(HALF):
                            tile = hg * HALF + j
                            pool.indirect_dma_start(
                                out=sender[:, hg % 4, j, :], out_offset=None, in_=t["table"],
                                in_offset=bass.IndirectOffsetOnAxis(ap=src_index[:, tile:tile + 1], axis=0),
                            ).then_inc(e_gather[hg % 4], 16)

                @block.tensor
                def _(pe):
                    def mlp1(g):
                        if g >= NGROUP:
                            return
                        s, b = divmod(g, SUPER // GROUP)
                        if b == 0:
                            pe.wait_ge(e_feats[s % 2], 16 * (s // 2 + 1))
                        if g:
                            pe.wait_ge(e_h1, g)
                        pe.matmul(p1_bank[:], a1[:, b * P:(b + 1) * P], feats[:, s % 2, :],
                                  start=True, stop=True).then_inc(e_p1, 1)

                    def mlp2(g):
                        if g >= NGROUP:
                            return
                        pe.wait_ge(e_h1, g + 1)
                        if g:
                            pe.wait_ge(e_h2, g)
                        pe.matmul(p2_bank[:], a2[:], h1[:, g % 2, :], start=True, stop=True).then_inc(e_p2, 1)

                    def mlp3(hg):
                        if hg >= NHALF:
                            return
                        g, half = divmod(hg, 2)
                        if half == 0:
                            pe.wait_ge(e_h2, g + 1)
                        if hg >= 3:
                            pe.wait_ge(e_msg, hg - 2)
                        for j in range(HALF):
                            channels = slice(64 * half, 64 * half + 64)
                            last = pe.matmul(weight_bank[hg % 3][:, j * P:(j + 1) * P],
                                             h2[channels, g % 2, j * P:(j + 1) * P],
                                             a3[channels, :], start=True, stop=True)
                        last.then_inc(e_w, 1)

                    def sum_receivers(hg):
                        g, half = divmod(hg, 2)
                        bank = acc_bank[g % 2]
                        if half == 0:
                            if g >= 2:
                                pe.wait_ge(e_acc, g - 1)
                            pe.matmul(bank[:, 0:3 * GWIDTH], zeros[:, 0:P], zeros[:], start=True, stop=False,
                                      skip_group_check=True)
                        pe.wait_ge(e_sel, hg + 1)
                        pe.wait_ge(e_msg, hg + 1)
                        for j in range(HALF):
                            tile = hg * HALF + j
                            off = int(BASE[tile] - BASE[g * GROUP])
                            m = msg[:, hg % 2, j]
                            sel = select[:, hg % 2, j]
                            pe.matmul(bank[:, off:off + WIN], m[:, 0:4, :], sel[:, 0, :],
                                      start=False, stop=False, skip_group_check=True)
                            for i in range(3):
                                lo = GWIDTH * (1 + i // 2) + off
                                last = pe.matmul(bank[64 * (i % 2):64 * (i % 2) + 64, lo:lo + WIN],
                                                 m[:, PAIR[i]:PAIR[i] + 2, :], sel[:, i + 1, :],
                                                 start=False, stop=(half == 1 and j == HALF - 1 and i == 2),
                                                 skip_group_check=True)
                        last.then_inc(e_half, 1)

                    for g in range(3):
                        mlp1(g)
                        if g >= 1:
                            mlp2(g - 1)
                    for hg in range(2):
                        mlp3(hg)
                    for g in range(NGROUP):
                        mlp1(g + 3)
                        mlp2(g + 2)
                        for half in range(2):
                            mlp3(2 * g + 2 + half)
                            sum_receivers(2 * g + half)

                @block.scalar
                def _(act_e):
                    def silu1(g):
                        if g >= NGROUP:
                            return
                        act_e.wait_ge(e_p1, g + 1)
                        if g >= 2:
                            act_e.wait_ge(e_p2, g - 1)
                        act_e.activation(h1[:, g % 2, :], p1_bank[:], ACT.Silu, bias=b12[:, 0:1]).then_inc(e_h1, 1)

                    def silu2(g):
                        if g >= NGROUP:
                            return
                        act_e.wait_ge(e_p2, g + 1)
                        if g >= 2:
                            act_e.wait_ge(e_w, 2 * (g - 1))
                        act_e.activation(h2[:, g % 2, :], p2_bank[:], ACT.Silu, bias=b12[:, 1:2]).then_inc(e_h2, 1)

                    silu1(0)
                    for g in range(NGROUP):
                        silu1(g + 1)
                        silu2(g)

                @block.vector
                def _(dve):
                    dve.tensor_tensor(rel[:], dst[:], base_row[:], ALU.subtract).then_inc(e_rel, 1)
                    dve.wait_ge(e_rel, 1)

                    def selections(hg):
                        if hg >= NHALF:
                            return
                        if hg >= 2:
                            dve.wait_ge(e_half, hg - 1)
                        for j in range(HALF):
                            tile = hg * HALF + j
                            for k in range(4):
                                last = dve.tensor_scalar(select[:, hg % 2, j, k, :], node_iota[:],
                                                         rel[:, tile:tile + 1], attr[:, k, tile:tile + 1],
                                                         ALU.is_equal, ALU.mult)
                        last.then_inc(e_sel, 1)

                    def messages(hg):
                        dve.wait_ge(e_w, hg + 1)
                        dve.wait_ge(e_gather[hg % 4], 16 * HALF * (hg // 4 + 1))
                        m = msg[:, hg % 2]
                        w = weight_bank[hg % 3][:].rearrange("p (j v u) -> p j v u", j=HALF, v=4)
                        row = sender[:, hg % 4].rearrange("p j (k u) -> p j k u", k=4)
                        dve.tensor_tensor(m[:, :, 0, :], row[:, :, 0, :], w[:, :, 0, :], ALU.mult)
                        dve.tensor_tensor(m[:, :, 5:8:2, :], row[:, :, 0:1, :].to_broadcast([P, HALF, 2, MUL]),
                                          w[:, :, 1:2, :].to_broadcast([P, HALF, 2, MUL]), ALU.mult)
                        dve.tensor_tensor(m[:, :, 1:4, :], row[:, :, 1:4, :],
                                          w[:, :, 2:3, :].to_broadcast([P, HALF, 3, MUL]), ALU.mult)
                        last = dve.tensor_tensor(m[:, :, 4:9:2, :], row[:, :, 1:4, :],
                                                 w[:, :, 3:4, :].to_broadcast([P, HALF, 3, MUL]), ALU.mult)
                        last.then_inc(e_msg, 1)

                    def add_group(g):
                        dve.wait_ge(e_half, 2 * g + 2)
                        if g:
                            dve.wait_ge(e_group, g)
                        at = int(BASE[g * GROUP])
                        dve.tensor_tensor(acc[:, 0:2, at:at + GWIDTH], acc[:, 0:2, at:at + GWIDTH],
                                          acc_bank[g % 2][:, 0:2 * GWIDTH].rearrange("p (a n) -> p a n", a=2),
                                          ALU.add).then_inc(e_group, 1)
                        dve.tensor_tensor(acc[0:64, 2, at:at + GWIDTH], acc[0:64, 2, at:at + GWIDTH],
                                          acc_bank[g % 2][0:64, 2 * GWIDTH:3 * GWIDTH], ALU.add).then_inc(e_acc, 1)
                        dve.wait_ge(e_acc, g + 1)

                    selections(0)
                    for hg in range(NHALF):
                        messages(hg)
                        selections(hg + 1)
                        if hg % 2 == 0 and hg:
                            add_group(hg // 2 - 1)
                    add_group(NGROUP - 1)
                    dve.tensor_scalar(dst[:], dst[:], -float(WIN), None, ALU.add).then_inc(e_rel, 1)
                    dve.wait_ge(e_rel, 2)
                    dve.tensor_scalar(wrap[:], dst[:], 0.0, float(TURN), ALU.is_lt, ALU.mult).then_inc(e_rel, 1)
                    dve.wait_ge(e_rel, 3)
                    dve.tensor_tensor(dst[:], dst[:], wrap[:], ALU.add).then_inc(e_rel, 1)
                    dve.wait_ge(e_rel, 4)

            with nc.Block() as block:
                @block.sync
                def _(sp):
                    turned = t["turned"].rearrange("(p a) n -> p a n", p=P)
                    with sp.If(rounds > 1):
                        sp.dma_start(turned, acc[:]).then_inc(e_turn, 16)
                        sp.wait_ge(e_turn, 16)
                        sp.dma_start(acc[:, :, 0:TURN - WIN], turned[:, :, WIN:TURN]).then_inc(e_turn, 16)
                        sp.dma_start(acc[:, :, TURN - WIN:TURN], turned[:, :, 0:WIN]).then_inc(e_turn, 16)
                        sp.wait_ge(e_turn, 48)
            with nc.Block() as block:
                @block.gpsimd
                def _(pool):
                    with pool.If(rounds > 1):
                        pool.dma_reset(range(e_gather[0].num, e_gather[3].num + 1))
                        for s in e_sems:
                            pool.sem_clear(s)

        f_po, f_sum, f_mom, f_sqrt, f_rstd, f_norm, f_st, f_out, f_w = (sem(n) for n in (
            "f_po", "f_sum", "f_mom", "f_sqrt", "f_rstd", "f_norm", "f_st", "f_out", "f_w"))
        scale = float(1 / np.sqrt(np.float32(2 * MUL))) / 10.0
        with nc.Block() as block:
            @block.tensor
            def _(pe):
                pe.wait_ge(f_w, 3)
                for n in range(NODE_TILES):
                    if n >= 4:
                        pe.wait_ge(f_sum, 2 * (n - 3))
                    out, c0 = banks[n % 4], n * P
                    c1 = min(c0 + P, TURN)
                    pe.matmul(out[:, 0:P], acc[:, 0, c0:c1], w_out[:, 0:P], start=True, stop=False)
                    pe.matmul(out[:, 0:P], acc[:, 1, c0:c1], w_out[:, P:2 * P], start=False, stop=False)
                    pe.matmul(out[:, 0:P], acc[0:64, 2, c0:c1], w_out[0:64, 2 * P:3 * P],
                              start=False, stop=True).then_inc(f_po, 1)

            @block.vector
            def _(dve):
                for row, col in ((0, P), (64, P), (MUL, 2 * P)):
                    view = w_out[row:row + MUL, col:col + P]
                    dve.tensor_scalar(view, view, float(1 / np.sqrt(np.float32(3))), None, ALU.mult).then_inc(f_w, 1)
                for n in range(NODE_TILES):
                    dve.wait_ge(f_po, n + 1)
                    out = banks[n % 4]
                    dve.scalar_tensor_tensor(x1[:, n, 0:MUL], out[:, 0:MUL], scale, x1[:, n, 0:MUL],
                                             ALU.mult, ALU.add).then_inc(f_sum, 1)
                    dve.scalar_tensor_tensor(x1[:, n, MUL:].rearrange("p (u i) -> p u i", i=3),
                                             out[:, MUL:P].rearrange("p (i u) -> p u i", i=3), scale,
                                             x1[:, n, MUL:].rearrange("p (u i) -> p u i", i=3),
                                             ALU.mult, ALU.add).then_inc(f_sum, 1)
                    dve.wait_ge(f_sum, 2 * n + 2)
                    dve.bn_stats(stats[:, n, :], x1[:, n, :]).then_inc(f_st, 1)
                    dve.wait_ge(f_st, n + 1)
                    dve.bn_aggr(moments[:, n, :], stats[:, n, :]).then_inc(f_mom, 1)
                dve.wait_ge(f_sqrt, 1)
                dve.reciprocal(rstd[:], rstd[:]).then_inc(f_rstd, 1)
                dve.wait_ge(f_rstd, 1)
                for n in range(NODE_TILES):
                    dve.tensor_scalar(x1[:, n, :], x1[:, n, :], moments[:, n, 0:1], rstd[:, n:n + 1],
                                      ALU.subtract, ALU.mult).then_inc(f_norm, 1)

            @block.scalar
            def _(act_e):
                act_e.wait_ge(f_mom, NODE_TILES)
                act_e.activation(rstd[:], moments[:, :, 1], ACT.Sqrt, bias=eps[:]).then_inc(f_sqrt, 1)

            @block.sync
            def _(sp):
                step, full = 12, NODE_TILES - 1
                for n in range(0, full, step):
                    sp.wait_ge(f_norm, n + step)
                    sp.dma_start(t["out"][n * P:(n + step) * P, :].rearrange("(a p) d -> p a d", p=P),
                                 x1[:, n:n + step, :]).then_inc(f_out, 16)
                sp.wait_ge(f_norm, NODE_TILES)
                sp.dma_start(t["out"][full * P:NODES, :], x1[0:LAST_ROWS, full, :]).then_inc(f_out, 16)
                sp.wait_ge(f_out, 16 * (full // step + 1))


def lay_out(i):
    a = {}
    a["x"] = i["x"]
    pad = NODE_COLS - NODES
    a["x_nodes"] = np.pad(i["x"], ((0, pad), (0, 0))).reshape(NODE_TILES, P, DIM).transpose(1, 0, 2)
    a["x_nodes"] = a["x_nodes"].reshape(P, NODE_TILES * DIM)
    a["seq_index"] = (np.pad(i["dst"].reshape(NODES, STEPS), ((0, pad), (0, 0)))
                      .reshape(NODE_TILES, P, STEPS).transpose(1, 0, 2).reshape(P, NODE_TILES * STEPS))
    epad = EDGE_TILES * P - EDGES
    a["dst"] = np.pad(i["dst"], (0, epad), constant_values=FAR).reshape(EDGE_TILES, P).T
    a["src"] = np.pad(i["src"], (0, epad)).reshape(EDGE_TILES, P).T
    a["attr4"] = (np.pad(i["edge_attr_4"], ((0, epad), (0, 0))).reshape(EDGE_TILES, P, 4)
                  .transpose(1, 2, 0).reshape(P, 4 * EDGE_TILES))
    a["attr8"] = (np.pad(i["edge_attr_8"], ((0, epad), (0, 0)))
                  .reshape(EDGE_TILES // SUPER, SUPER // GROUP, 2, HALF, P, 8)
                  .transpose(0, 1, 2, 5, 3, 4).reshape(EDGE_TILES // SUPER, P, HALF * P))
    a["w_ih"] = i["L0_gnn_w_ih"].T
    a["w_hh"] = i["L0_gnn_w_hh"].T
    a["bias2"] = np.concatenate([i["L0_gnn_b_ih"].reshape(4, HID).T, i["L0_gnn_b_hh"].reshape(4, HID).T], axis=1)
    a["w_lin"] = i["L0_gnn_w_lin"].T
    a["b_lin"] = i["L0_gnn_b_lin"].reshape(1, HID)
    up = np.zeros((P, P), np.float32)
    up[0:MUL, 0:MUL] = i["L1_gnn_W_up_s"]
    for k in range(3):
        up[MUL + k::3, MUL * (k + 1):MUL * (k + 2)] = i["L1_gnn_W_up_v"]
    a["w_up"] = up
    a1 = np.zeros((P, GROUP, 2, 64), np.float32)
    a2 = np.zeros((P, P), np.float32)
    for b in range(GROUP):
        for r in range(2):
            a1[16 * b + 8 * r:16 * b + 8 * r + 8, b, r] = i["L1_gnn_A1"]
    for r in range(2):
        a2[64 * r:64 * r + 64, 64 * r:64 * r + 64] = i["L1_gnn_A2"]
    a["a1"] = a1.reshape(P, GROUP * P)
    a["a2"] = a2
    a["a3"] = np.concatenate([i["L1_gnn_A3"], i["L1_gnn_A3"]])
    a["b12"] = np.stack([np.concatenate([i["L1_gnn_b1"]] * 2), np.concatenate([i["L1_gnn_b2"]] * 2)], axis=1)
    ws, wv = i["L1_gnn_W_out_s"], i["L1_gnn_W_out_v"]
    w = np.zeros((3, P, P), np.float32)
    w[0, 0:MUL, 0:MUL] = ws[0:MUL]
    for k in range(3):
        cols = slice(MUL * (k + 1), MUL * (k + 2))
        w[0, cols, cols] = wv[MUL:]
        s3, v1 = (64 * k, 64 * k + MUL) if k < 2 else (MUL, 0)
        w[1 + k // 2, s3:s3 + MUL, 0:MUL] = ws[MUL:]
        w[1 + k // 2, v1:v1 + MUL, cols] = wv[0:MUL]
    a["w_out"] = w.transpose(1, 0, 2).reshape(P, 3 * P)
    a["ident"] = np.eye(P, dtype=np.float32)
    a["base_row"] = np.broadcast_to(BASE.astype(np.float32), (P, EDGE_TILES))
    a["node_iota"] = np.broadcast_to(np.arange(WIN, dtype=np.float32), (P, WIN))
    return {k: np.ascontiguousarray(v) for k, v in a.items()}


def kernel(**inputs):
    import concourse.bacc as bacc
    from concourse.bass_utils import run_bass_kernel_spmd

    arrays = lay_out({k: np.asarray(v) for k, v in inputs.items()})
    nc = bacc.Bacc("TRN2", target_bir_lowering=False, num_devices=1)
    t = {k: nc.dram_tensor(k + "_in", v.shape, mybir.dt.from_np(v.dtype), kind="ExternalInput").ap()
         for k, v in arrays.items()}
    t["table"] = nc.dram_tensor("table", (NODE_COLS, P), F32, kind="Internal").ap()
    t["turned"] = nc.dram_tensor("turned", (3 * P, TURN), F32, kind="Internal").ap()
    t["out"] = nc.dram_tensor("out", (NODES, DIM), F32, kind="ExternalOutput").ap()
    build(nc, t)
    result = run_bass_kernel_spmd(nc, [{k + "_in": v for k, v in arrays.items()}], core_ids=[0])
    return result.results[0]["out"]
```

```python
from contextlib import ExitStack

import numpy as np

import concourse.bass as bass
from concourse import mybir

F32 = mybir.dt.float32
I32 = mybir.dt.int32
BF16 = mybir.dt.bfloat16
ALU = mybir.AluOpType
ACT = mybir.ActivationFunctionType

P = 128
NODES, DIM, HID = 6250, 128, 128
EDGES = 106250
STEPS = EDGES // NODES
MUL = 32
NODE_TILES = -(-NODES // P)
NODE_COLS = NODE_TILES * P
LAST_ROWS = NODES - (NODE_TILES - 1) * P

CHUNK = 512
CHUNKS = [(c, min(CHUNK, NODE_COLS - c)) for c in range(0, NODE_COLS, CHUNK)]
NCH = len(CHUNKS)
WORK = [(t, c) for t in range(STEPS) for c in range(NCH)]
GATES = (0, 2, 1, 3)

GROUP = 8
HALF = GROUP // 2
SUPER = 64
EDGE_TILES = -(-(-(-EDGES // P)) // SUPER) * SUPER
NGROUP = EDGE_TILES // GROUP
WIN = 80
ROUNDS = -(-NODES // WIN)
TURN = ROUNDS * WIN
FAR = 1 << 24


DVE_FACTORS = 2

PAIR = (4, 6, 7)


def window_bases():
    centre = (np.arange(EDGE_TILES) + 0.5) * P * NODES / EDGES
    base = np.clip(np.rint(centre - WIN / 2), 0, None).astype(int)
    width = max(base[g * GROUP + GROUP - 1] - base[g * GROUP] for g in range(NGROUP)) + WIN
    width += width % 2
    base = np.minimum(base, TURN - width)
    return base, width


BASE, GWIDTH = window_bases()


def build(nc, t):
    ctx = ExitStack()
    with ctx:
        def sb(name, shape, dt=F32, scope=ctx):
            return scope.enter_context(nc.sbuf_tensor(name, shape, dt))

        def ps(name, shape, dt=F32, scope=ctx):
            return scope.enter_context(nc.psum_tensor(name, shape, dt))

        def sem(name):
            return ctx.enter_context(nc.semaphore(name))

        x1 = sb("x1", [P, NODE_TILES, DIM])
        dst = sb("dst", [P, EDGE_TILES])
        rel = sb("rel", [P, EDGE_TILES])
        base_row = sb("base_row", [P, EDGE_TILES])
        src_index = sb("src_index", [P, EDGE_TILES], I32)
        attr = sb("attr", [P, 4, EDGE_TILES])
        node_iota = sb("node_iota", [P, WIN])
        ones = sb("ones", [P, P])
        ident = sb("ident", [P, P])
        eps = sb("eps", [P, 1])
        w_up = sb("w_up", [P, P])
        a1 = sb("a1", [P, GROUP * P])
        a2 = sb("a2", [P, P])
        a3 = sb("a3", [P, P])
        b12 = sb("b12", [P, 2])
        w_out = sb("w_out", [P, 3 * P])
        w_lin = sb("w_lin", [P, P])
        b_lin = sb("b_lin", [1, P])
        rounds_word = sb("rounds_word", [1, 1], I32)
        zeros = sb("zeros", [P, 3 * GWIDTH], BF16)
        stats = sb("stats", [P, NODE_TILES, 6])
        moments = sb("moments", [P, NODE_TILES, 2])
        rstd = sb("rstd", [P, NODE_TILES])

        banks = [ps(f"bank{i}", [P, 512]) for i in range(8)]

        s_const = sem("s_const")
        s_wait = [sem(f"s_gather{i}") for i in range(4)]

        with ExitStack() as scope:
            w_ih = sb("w_ih", [P, 4 * HID], scope=scope)
            w_hh = sb("w_hh", [P, 4 * HID], scope=scope)
            bias2 = sb("bias2", [P, 2, 4 * HID], scope=scope)
            seq_index = sb("seq_index", [P, NODE_TILES * STEPS], I32, scope=scope)
            dst_int = sb("dst_int", [P, EDGE_TILES], I32, scope=scope)
            inside = sb("inside", [P, EDGE_TILES], scope=scope)
            inside2 = sb("inside2", [P, EDGE_TILES], scope=scope)
            count = sb("count", [P, 1], scope=scope)
            missed = sb("missed", [1, 1], scope=scope)
            hidden = sb("hidden", [P, NODE_COLS], scope=scope)
            x_t = hidden
            cell = sb("cell", [P, NODE_COLS], scope=scope)
            rows = sb("rows", [P, 4, 4, 4 * HID], scope=scope)
            act = sb("act", [P, 2, 4, CHUNK], scope=scope)
            tanh_c = sb("tanh_c", [P, 2, CHUNK], scope=scope)
            prod_ig = sb("prod_ig", [P, CHUNK], scope=scope)
            prod_fc = sb("prod_fc", [P, CHUNK], scope=scope)

            s_wts, s_idx, s_rest = sem("s_wts"), sem("s_idx"), sem("s_rest")
            s_xt = [sem(f"s_xt{i}") for i in range(4)]
            s_in, s_row, s_sumb, s_set = sem("s_in"), sem("s_row"), sem("s_sumb"), sem("s_set")
            s_store = [sem(f"s_store{i}") for i in range(8)]
            s_gate, s_act = sem("s_gate"), sem("s_act")
            s_cell, s_tanh, s_hidden = sem("s_cell"), sem("s_tanh"), sem("s_hidden")
            s_ig, s_fc, s_prep, s_count = sem("s_ig"), sem("s_fc"), sem("s_prep"), sem("s_count")

            xt_parts = np.array_split(np.arange(NODE_TILES), 4)
            in_rows = rows[:].rearrange("p a b n -> p (a b) n")
            with nc.Block() as block:
                @block.sync
                def _(sp):
                    for tile, name in ((w_ih, "w_ih"), (bias2, "bias2")):
                        view = tile[:] if tile is w_ih else tile[:].rearrange("p a n -> p (a n)")
                        sp.dma_start(view, t[name]).then_inc(s_wts, 16)
                    for i, part in enumerate(xt_parts):
                        cols = slice(int(part[0]) * P, int(part[-1] + 1) * P)
                        sp.dma_start(x_t[:, cols], t["x_t"][:, cols]).then_inc(s_xt[i], 16)
                    for tile, name in ((w_hh, "w_hh"), (ident, "ident"), (seq_index, "seq_index")):
                        sp.dma_start(tile[:], t[name]).then_inc(s_idx, 16)
                    for n in range(NODE_TILES):
                        sp.wait_ge(s_row, n + 1)
                        sp.dma_start(t["gates"][n * P:(n + 1) * P, :], in_rows[:, n % 8, :]).then_inc(s_store[n % 8], 16)
                    for i in range(8):
                        sp.wait_ge(s_store[i], 16 * len(range(i, NODE_TILES, 8)))

                @block.gpsimd
                def _(pool):
                    pool.memset(ones[:], 1.0)
                    pool.memset(eps[:], 1e-5)
                    pool.memset(zeros[:], 0.0).then_inc(s_set, 1)
                    pool.wait_ge(s_set, 1)

                @block.tensor
                def _(pe):
                    pe.wait_ge(s_wts, 32)
                    for i, part in enumerate(xt_parts):
                        pe.wait_ge(s_xt[i], 16)
                        for n in map(int, part):
                            if n >= 8:
                                pe.wait_ge(s_row, n - 7)
                            pe.matmul(banks[n % 8][:], x_t[:, n * P:(n + 1) * P], w_ih[:],
                                      start=True, stop=True).then_inc(s_in, 1)

                @block.vector
                def _(dve):
                    dve.wait_ge(s_wts, 32)
                    dve.tensor_tensor(bias2[:, 0, :], bias2[:, 0, :], bias2[:, 1, :], ALU.add).then_inc(s_sumb, 1)
                    dve.wait_ge(s_sumb, 1)
                    for n in range(NODE_TILES):
                        dve.wait_ge(s_in, n + 1)
                        if n >= 8:
                            dve.wait_ge(s_store[n % 8], 16 * (n // 8))
                        dve.tensor_tensor(in_rows[:, n % 8, :], banks[n % 8][:], bias2[:, 0, :],
                                          ALU.add).then_inc(s_row, 1)

            with nc.Block() as block:
                @block.sync
                def _(sp):
                    sp.dma_start(dst_int[:], t["dst"]).then_inc(s_const, 16)
                    sp.dma_start(base_row[:], t["base_row"]).then_inc(s_const, 16)
                    sp.dma_start(node_iota[:], t["node_iota"]).then_inc(s_rest, 16)
                    sp.dma_start(x1[:].rearrange("p a d -> p (a d)"), t["x_nodes"]).then_inc(s_rest, 16)
                    sp.dma_start(src_index[:], t["src"]).then_inc(s_rest, 16)
                    sp.dma_start(attr[:].rearrange("p k e -> p (k e)"), t["attr4"]).then_inc(s_rest, 16)
                    for tile, name in ((w_up, "w_up"), (a1, "a1"), (a2, "a2"), (a3, "a3"), (b12, "b12"),
                                       (w_out, "w_out"), (w_lin, "w_lin"), (b_lin, "b_lin")):
                        sp.dma_start(tile[:], t[name]).then_inc(s_rest, 16)
                    sp.wait_ge(s_rest, 16 * 12)

                @block.gpsimd
                def _(pool):
                    pool.wait_ge(s_idx, 48)
                    for k, (step, c) in enumerate(WORK):
                        if k >= 4:
                            pool.wait_ge(s_gate, 4 * (k - 3))
                        c0, width = CHUNKS[c]
                        for j in range(width // P):
                            col = (c0 // P + j) * STEPS + step
                            pool.indirect_dma_start(
                                out=rows[:, k % 4, j, :], out_offset=None, in_=t["gates"],
                                in_offset=bass.IndirectOffsetOnAxis(ap=seq_index[:, col:col + 1], axis=0),
                            ).then_inc(s_wait[k % 4], 16)

                @block.tensor
                def _(pe):
                    landed = [0] * 4
                    pe.wait_ge(s_idx, 48)
                    for k, (step, c) in enumerate(WORK):
                        c0, width = CHUNKS[c]
                        landed[k % 4] += 16 * (width // P)
                        pe.wait_ge(s_wait[k % 4], landed[k % 4])
                        for q, gate in enumerate(GATES):
                            n = 4 * k + q
                            if n >= 8:
                                pe.wait_ge(s_act, n - 7)
                            bank, cols = banks[n % 8], slice(gate * HID, (gate + 1) * HID)
                            for j in range(width // P):
                                last = pe.matmul(bank[:, j * P:(j + 1) * P], rows[:, k % 4, j, cols], ident[:],
                                                 is_transpose=True, start=(j == 0), stop=False,
                                                 skip_group_check=True)
                            if step and q == 0:
                                pe.wait_ge(s_hidden, k - NCH + 1)
                            if step:
                                last = pe.matmul(bank[:, 0:width], w_hh[:, cols], hidden[:, c0:c0 + width],
                                                 start=False, stop=True, skip_group_check=True)
                            last.then_inc(s_gate, 1)
                    pe.wait_ge(s_prep, 5)
                    pe.matmul(banks[0][0:1, 0:1], count[:], ones[:, 0:1], start=True, stop=True).then_inc(s_count, 1)

                @block.scalar
                def _(act_e):
                    def tanh_cell(k):
                        c0, width = CHUNKS[WORK[k][1]]
                        act_e.wait_ge(s_cell, k + 1)
                        if k >= 2:
                            act_e.wait_ge(s_hidden, k - 1)
                        act_e.activation(tanh_c[:, k % 2, 0:width], cell[:, c0:c0 + width],
                                         ACT.Tanh).then_inc(s_tanh, 1)

                    for k, (step, c) in enumerate(WORK):
                        width = CHUNKS[c][1]
                        for q, gate in enumerate(GATES):
                            n = 4 * k + q
                            if q == 0 and k >= 2:
                                act_e.wait_ge(s_hidden, k - 1)
                            act_e.wait_ge(s_gate, n + 1)
                            act_e.activation(act[:, k % 2, gate, 0:width], banks[n % 8][:, 0:width],
                                             ACT.Tanh if gate == 2 else ACT.Sigmoid).then_inc(s_act, 1)
                        if k:
                            tanh_cell(k - 1)
                    tanh_cell(len(WORK) - 1)

                @block.vector
                def _(dve):
                    def new_hidden(k):
                        c0, width = CHUNKS[WORK[k][1]]
                        dve.wait_ge(s_tanh, k + 1)
                        dve.tensor_tensor(hidden[:, c0:c0 + width], act[:, k % 2, 3, 0:width],
                                          tanh_c[:, k % 2, 0:width], ALU.mult).then_inc(s_hidden, 1)

                    for k, (step, c) in enumerate(WORK):
                        c0, width = CHUNKS[c]
                        if k:
                            new_hidden(k - 1)
                        here = cell[:, c0:c0 + width]
                        gates = act[:, k % 2, :, 0:width]
                        dve.wait_ge(s_act, 4 * k + 2)
                        if step == 0:
                            dve.tensor_tensor(here, gates[:, 0], gates[:, 2], ALU.mult).then_inc(s_cell, 1)
                            dve.wait_ge(s_act, 4 * k + 4)
                            continue
                        n = k - NCH + 1
                        dve.wait_ge(s_cell, k)
                        dve.tensor_tensor(prod_ig[:, 0:width], gates[:, 0], gates[:, 2], ALU.mult).then_inc(s_ig, 1)
                        dve.wait_ge(s_act, 4 * k + 3)
                        dve.tensor_tensor(prod_fc[:, 0:width], gates[:, 1], here, ALU.mult).then_inc(s_fc, 1)
                        dve.wait_ge(s_ig, n)
                        dve.wait_ge(s_fc, n)
                        dve.tensor_tensor(here, prod_ig[:, 0:width], prod_fc[:, 0:width], ALU.add).then_inc(s_cell, 1)
                        dve.wait_ge(s_act, 4 * k + 4)
                    new_hidden(len(WORK) - 1)
                    dve.wait_ge(s_const, 32)
                    dve.tensor_copy(dst[:], dst_int[:]).then_inc(s_prep, 1)
                    dve.wait_ge(s_prep, 1)
                    dve.tensor_tensor(rel[:], dst[:], base_row[:], ALU.subtract).then_inc(s_prep, 1)
                    dve.wait_ge(s_prep, 2)
                    dve.tensor_scalar(inside[:], rel[:], 0.0, None, ALU.is_ge).then_inc(s_prep, 1)
                    dve.wait_ge(s_prep, 3)
                    dve.scalar_tensor_tensor(inside2[:], rel[:], float(WIN), inside[:], ALU.is_lt,
                                             ALU.mult).then_inc(s_prep, 1)
                    dve.wait_ge(s_prep, 4)
                    dve.tensor_reduce(count[:], inside2[:], mybir.AxisListType.X, ALU.add).then_inc(s_prep, 1)
                    dve.wait_ge(s_count, 1)
                    dve.tensor_scalar(missed[:], banks[0][0:1, 0:1], float(EDGES), float(ROUNDS - 1),
                                      ALU.is_lt, ALU.mult).then_inc(s_prep, 1)
                    dve.wait_ge(s_prep, 6)
                    dve.tensor_scalar(rounds_word[:], missed[:], 1.0, None, ALU.add).then_inc(s_prep, 1)
                    dve.wait_ge(s_prep, 7)

            x1t = sb("x1t", [P, 2, P], scope=scope)
            up = sb("up", [P, 4, P], scope=scope)
            s_po, s_sum, s_mom, s_sqrt, s_rstd, s_norm = (sem(n) for n in (
                "s_po", "s_sum", "s_mom", "s_sqrt", "s_rstd", "s_norm"))
            s_st, s_x1t, s_x1c, s_upp, s_up = (sem(n) for n in ("s_st", "s_x1t", "s_x1c", "s_upp", "s_up"))
            s_table = [sem(f"s_table{i}") for i in range(4)]
            with nc.Block() as block:
                @block.tensor
                def _(pe):
                    for n in range(NODE_TILES):
                        if n >= 4:
                            pe.wait_ge(s_sum, n - 3)
                        out = banks[n % 4][:, 0:P]
                        pe.matmul(out, hidden[:, n * P:(n + 1) * P], w_lin[:], start=True, stop=False)
                        pe.matmul(out, ones[0:1, :], b_lin[:], start=False, stop=True).then_inc(s_po, 1)
                    for n in range(NODE_TILES):
                        pe.wait_ge(s_norm, n + 1)
                        if n >= 2:
                            pe.wait_ge(s_x1c, n - 1)
                        pe.transpose(banks[4 + n % 2][:, 0:P], x1[:, n, :], ident[:]).then_inc(s_x1t, 1)
                        pe.wait_ge(s_x1c, n + 1)
                        if n >= 2:
                            pe.wait_ge(s_up, n - 1)
                        pe.matmul(banks[6 + n % 2][:, 0:P], x1t[:, n % 2, :], w_up[:],
                                  start=True, stop=True).then_inc(s_upp, 1)

                @block.vector
                def _(dve):
                    for n in range(NODE_TILES):
                        dve.wait_ge(s_po, n + 1)
                        dve.tensor_tensor(x1[:, n, :], banks[n % 4][:, 0:P], x1[:, n, :], ALU.add).then_inc(s_sum, 1)
                        dve.wait_ge(s_sum, n + 1)
                        dve.bn_stats(stats[:, n, :], x1[:, n, :]).then_inc(s_st, 1)
                        dve.wait_ge(s_st, n + 1)
                        dve.bn_aggr(moments[:, n, :], stats[:, n, :]).then_inc(s_mom, 1)
                    dve.wait_ge(s_sqrt, 1)
                    dve.reciprocal(rstd[:], rstd[:]).then_inc(s_rstd, 1)
                    dve.wait_ge(s_rstd, 1)
                    for n in range(NODE_TILES):
                        dve.tensor_scalar(x1[:, n, :], x1[:, n, :], moments[:, n, 0:1], rstd[:, n:n + 1],
                                          ALU.subtract, ALU.mult).then_inc(s_norm, 1)

                def projected(act_e, n):
                    act_e.wait_ge(s_upp, n + 1)
                    if n >= 4:
                        act_e.wait_ge(s_table[n % 4], 16 * (n // 4))
                    act_e.activation(up[:, n % 4, :], banks[6 + n % 2][:, 0:P], ACT.Copy,
                                     scale=float(1 / np.sqrt(np.float32(MUL)))).then_inc(s_up, 1)

                @block.scalar
                def _(act_e):
                    act_e.wait_ge(s_mom, NODE_TILES)
                    act_e.activation(rstd[:], moments[:, :, 1], ACT.Sqrt, bias=eps[:]).then_inc(s_sqrt, 1)
                    for n in range(NODE_TILES):
                        act_e.wait_ge(s_x1t, n + 1)
                        if n >= 2:
                            act_e.wait_ge(s_upp, n - 1)
                        act_e.activation(x1t[:, n % 2, :], banks[4 + n % 2][:, 0:P], ACT.Copy).then_inc(s_x1c, 1)
                        if n:
                            projected(act_e, n - 1)
                    projected(act_e, NODE_TILES - 1)

                @block.sync
                def _(sp):
                    for n in range(NODE_TILES):
                        sp.wait_ge(s_up, n + 1)
                        sp.dma_start(t["table"][n * P:(n + 1) * P, :], up[:, n % 4, :]).then_inc(s_table[n % 4], 16)
                    for i in range(4):
                        sp.wait_ge(s_table[i], 16 * len(range(i, NODE_TILES, 4)))

        acc = sb("acc", [P, 3, max(TURN, NODE_COLS)])
        feats = sb("feats", [P, 2, 512])
        h1 = sb("h1", [P, 2, 512])
        h2 = sb("h2", [P, 2, 512])
        sender = sb("sender", [P, 4, HALF, P])
        msg = sb("msg", [P, 2, HALF, 9, MUL])
        select = sb("select", [P, 2, HALF, 4, WIN])
        match = sb("match", [P, 2, HALF, WIN])
        wrap = sb("wrap", [P, EDGE_TILES])

        e_rel, e_zero, e_turn = sem("e_rel"), sem("e_zero"), sem("e_turn")
        e_feats = [sem("e_feats0"), sem("e_feats1")]
        e_gather = [sem(f"e_gather{i}") for i in range(4)]
        e_p1, e_h1, e_p2, e_h2, e_w = (sem(n) for n in ("e_p1", "e_h1", "e_p2", "e_h2", "e_w"))
        e_match, e_sel, e_sel2, e_msg, e_half, e_group, e_acc = (
            sem(n) for n in ("e_match", "e_sel", "e_sel2", "e_msg", "e_half", "e_group", "e_acc"))
        e_sems = [e_rel, e_zero, e_turn, *e_feats, *e_gather, e_p1, e_h1, e_p2, e_h2, e_w,
                  e_match, e_sel, e_sel2, e_msg, e_half, e_group, e_acc]
        p1_bank, p2_bank = banks[0], banks[1]
        weight_bank, acc_bank = banks[2:5], banks[5:7]
        NHALF = 2 * NGROUP

        with nc.Block() as block:
            @block.gpsimd
            def _(pool):
                pool.memset(acc[:].rearrange("p a b -> p (a b)"), 0.0).then_inc(e_zero, 1)
                pool.wait_ge(e_zero, 1)
                pool.sem_clear(e_zero)
        rounds = nc.values_load(rounds_word[0:1, 0:1], min_val=1, max_val=ROUNDS)

        with nc.Fori(0, rounds):
            with nc.Block() as block:
                @block.sync
                def _(sp):
                    for s in range(EDGE_TILES // SUPER):
                        if s >= 2:
                            sp.wait_ge(e_p1, GROUP * (s - 1))
                        sp.dma_start(feats[:, s % 2, :], t["attr8"][s]).then_inc(e_feats[s % 2], 16)

                @block.gpsimd
                def _(pool):
                    for hg in range(NHALF):
                        if hg >= 4:
                            pool.wait_ge(e_msg, hg - 3)
                        for j in range(HALF):
                            tile = hg * HALF + j
                            pool.indirect_dma_start(
                                out=sender[:, hg % 4, j, :], out_offset=None, in_=t["table"],
                                in_offset=bass.IndirectOffsetOnAxis(ap=src_index[:, tile:tile + 1], axis=0),
                            ).then_inc(e_gather[hg % 4], 16)

                @block.tensor
                def _(pe):
                    def mlp1(g):
                        if g >= NGROUP:
                            return
                        s, b = divmod(g, SUPER // GROUP)
                        if b == 0:
                            pe.wait_ge(e_feats[s % 2], 16 * (s // 2 + 1))
                        if g:
                            pe.wait_ge(e_h1, g)
                        pe.matmul(p1_bank[:], a1[:, b * P:(b + 1) * P], feats[:, s % 2, :],
                                  start=True, stop=True).then_inc(e_p1, 1)

                    def mlp2(g):
                        if g >= NGROUP:
                            return
                        pe.wait_ge(e_h1, g + 1)
                        if g:
                            pe.wait_ge(e_h2, g)
                        pe.matmul(p2_bank[:], a2[:], h1[:, g % 2, :], start=True, stop=True).then_inc(e_p2, 1)

                    def mlp3(hg):
                        if hg >= NHALF:
                            return
                        g, half = divmod(hg, 2)
                        if half == 0:
                            pe.wait_ge(e_h2, g + 1)
                        if hg >= 3:
                            pe.wait_ge(e_msg, hg - 2)
                        for j in range(HALF):
                            channels = slice(64 * half, 64 * half + 64)
                            last = pe.matmul(weight_bank[hg % 3][:, j * P:(j + 1) * P],
                                             h2[channels, g % 2, j * P:(j + 1) * P],
                                             a3[channels, :], start=True, stop=True)
                        last.then_inc(e_w, 1)

                    def sum_receivers(hg):
                        g, half = divmod(hg, 2)
                        bank = acc_bank[g % 2]
                        if half == 0:
                            if g >= 2:
                                pe.wait_ge(e_acc, g - 1)
                            pe.matmul(bank[:, 0:3 * GWIDTH], zeros[:, 0:P], zeros[:], start=True, stop=False,
                                      skip_group_check=True)
                        pe.wait_ge(e_sel, hg + 1)
                        pe.wait_ge(e_sel2, hg + 1)
                        pe.wait_ge(e_msg, hg + 1)
                        for j in range(HALF):
                            tile = hg * HALF + j
                            off = int(BASE[tile] - BASE[g * GROUP])
                            m = msg[:, hg % 2, j]
                            sel = select[:, hg % 2, j]
                            pe.matmul(bank[:, off:off + WIN], m[:, 0:4, :], sel[:, 0, :],
                                      start=False, stop=False, skip_group_check=True)
                            for i in range(3):
                                lo = GWIDTH * (1 + i // 2) + off
                                last = pe.matmul(bank[64 * (i % 2):64 * (i % 2) + 64, lo:lo + WIN],
                                                 m[:, PAIR[i]:PAIR[i] + 2, :], sel[:, i + 1, :],
                                                 start=False, stop=(half == 1 and j == HALF - 1 and i == 2),
                                                 skip_group_check=True)
                        last.then_inc(e_half, 1)

                    for g in range(3):
                        mlp1(g)
                        if g >= 1:
                            mlp2(g - 1)
                    for hg in range(2):
                        mlp3(hg)
                    for g in range(NGROUP):
                        mlp1(g + 3)
                        mlp2(g + 2)
                        for half in range(2):
                            mlp3(2 * g + 2 + half)
                            sum_receivers(2 * g + half)

                @block.scalar
                def _(act_e):
                    def silu1(g):
                        if g >= NGROUP:
                            return
                        act_e.wait_ge(e_p1, g + 1)
                        if g >= 2:
                            act_e.wait_ge(e_p2, g - 1)
                        act_e.activation(h1[:, g % 2, :], p1_bank[:], ACT.Silu, bias=b12[:, 0:1]).then_inc(e_h1, 1)

                    def silu2(g):
                        if g >= NGROUP:
                            return
                        act_e.wait_ge(e_p2, g + 1)
                        if g >= 2:
                            act_e.wait_ge(e_w, 2 * (g - 1))
                        act_e.activation(h2[:, g % 2, :], p2_bank[:], ACT.Silu, bias=b12[:, 1:2]).then_inc(e_h2, 1)

                    def selections(hg):
                        act_e.wait_ge(e_match, hg + 1)
                        if hg >= 2:
                            act_e.wait_ge(e_half, hg - 1)
                        for j in range(HALF):
                            tile = hg * HALF + j
                            for k in range(DVE_FACTORS, 4):
                                last = act_e.activation(select[:, hg % 2, j, k, :], match[:, hg % 2, j], ACT.Copy,
                                                        scale=attr[:, k, tile:tile + 1])
                        last.then_inc(e_sel2, 1)

                    for g in range(2):
                        silu1(g)
                    silu2(0)
                    silu1(2)
                    silu2(1)
                    for g in range(NGROUP):
                        selections(2 * g)
                        silu1(g + 3)
                        selections(2 * g + 1)
                        silu2(g + 2)

                @block.vector
                def _(dve):
                    dve.tensor_tensor(rel[:], dst[:], base_row[:], ALU.subtract).then_inc(e_rel, 1)
                    dve.wait_ge(e_rel, 1)

                    def selections(hg):
                        if hg >= NHALF:
                            return
                        if hg >= 2:
                            dve.wait_ge(e_half, hg - 1)
                            dve.wait_ge(e_sel2, hg - 1)
                        tiles = slice(hg * HALF, hg * HALF + HALF)
                        full = [P, HALF, WIN]
                        dve.tensor_tensor(match[:, hg % 2], node_iota[:].rearrange("p (a n) -> p a n", a=1).to_broadcast(full),
                                          rel[:, tiles].rearrange("p (j n) -> p j n", n=1).to_broadcast(full),
                                          ALU.is_equal).then_inc(e_match, 1)
                        dve.wait_ge(e_match, hg + 1)
                        for k in range(DVE_FACTORS):
                            last = dve.tensor_tensor(
                                select[:, hg % 2, :, k, :], match[:, hg % 2],
                                attr[:, k, tiles].rearrange("p (j n) -> p j n", n=1).to_broadcast(full), ALU.mult)
                        last.then_inc(e_sel, 1)

                    def messages(hg):
                        dve.wait_ge(e_w, hg + 1)
                        dve.wait_ge(e_gather[hg % 4], 16 * HALF * (hg // 4 + 1))
                        m = msg[:, hg % 2]
                        w = weight_bank[hg % 3][:].rearrange("p (j v u) -> p j v u", j=HALF, v=4)
                        row = sender[:, hg % 4].rearrange("p j (k u) -> p j k u", k=4)
                        dve.tensor_tensor(m[:, :, 0, :], row[:, :, 0, :], w[:, :, 0, :], ALU.mult)
                        dve.tensor_tensor(m[:, :, 5:8:2, :], row[:, :, 0:1, :].to_broadcast([P, HALF, 2, MUL]),
                                          w[:, :, 1:2, :].to_broadcast([P, HALF, 2, MUL]), ALU.mult)
                        dve.tensor_tensor(m[:, :, 1:4, :], row[:, :, 1:4, :],
                                          w[:, :, 2:3, :].to_broadcast([P, HALF, 3, MUL]), ALU.mult)
                        last = dve.tensor_tensor(m[:, :, 4:9:2, :], row[:, :, 1:4, :],
                                                 w[:, :, 3:4, :].to_broadcast([P, HALF, 3, MUL]), ALU.mult)
                        last.then_inc(e_msg, 1)

                    def add_group(g):
                        dve.wait_ge(e_half, 2 * g + 2)
                        if g:
                            dve.wait_ge(e_group, g)
                        at = int(BASE[g * GROUP])
                        dve.tensor_tensor(acc[:, 0:2, at:at + GWIDTH], acc[:, 0:2, at:at + GWIDTH],
                                          acc_bank[g % 2][:, 0:2 * GWIDTH].rearrange("p (a n) -> p a n", a=2),
                                          ALU.add).then_inc(e_group, 1)
                        dve.tensor_tensor(acc[0:64, 2, at:at + GWIDTH], acc[0:64, 2, at:at + GWIDTH],
                                          acc_bank[g % 2][0:64, 2 * GWIDTH:3 * GWIDTH], ALU.add).then_inc(e_acc, 1)
                        dve.wait_ge(e_acc, g + 1)

                    selections(0)
                    for hg in range(NHALF):
                        messages(hg)
                        selections(hg + 1)
                        if hg % 2 == 0 and hg:
                            add_group(hg // 2 - 1)
                    add_group(NGROUP - 1)
                    dve.tensor_scalar(dst[:], dst[:], -float(WIN), None, ALU.add).then_inc(e_rel, 1)
                    dve.wait_ge(e_rel, 2)
                    dve.tensor_scalar(wrap[:], dst[:], 0.0, float(TURN), ALU.is_lt, ALU.mult).then_inc(e_rel, 1)
                    dve.wait_ge(e_rel, 3)
                    dve.tensor_tensor(dst[:], dst[:], wrap[:], ALU.add).then_inc(e_rel, 1)
                    dve.wait_ge(e_rel, 4)

            with nc.Block() as block:
                @block.sync
                def _(sp):
                    turned = t["turned"].rearrange("(p a) n -> p a n", p=P)
                    with sp.If(rounds > 1):
                        sp.dma_start(turned, acc[:, :, 0:TURN]).then_inc(e_turn, 16)
                        sp.wait_ge(e_turn, 16)
                        sp.dma_start(acc[:, :, 0:TURN - WIN], turned[:, :, WIN:TURN]).then_inc(e_turn, 16)
                        sp.dma_start(acc[:, :, TURN - WIN:TURN], turned[:, :, 0:WIN]).then_inc(e_turn, 16)
                        sp.wait_ge(e_turn, 48)
            with nc.Block() as block:
                @block.gpsimd
                def _(pool):
                    with pool.If(rounds > 1):
                        pool.dma_reset(range(e_gather[0].num, e_gather[3].num + 1))
                        for s in e_sems:
                            pool.sem_clear(s)

        f_po, f_sum, f_mom, f_sqrt, f_rstd, f_norm, f_st, f_out, f_w = (sem(n) for n in (
            "f_po", "f_sum", "f_mom", "f_sqrt", "f_rstd", "f_norm", "f_st", "f_out", "f_w"))
        scale = float(1 / np.sqrt(np.float32(2 * MUL))) / 10.0
        with nc.Block() as block:
            @block.tensor
            def _(pe):
                pe.wait_ge(f_w, 3)
                for n in range(NODE_TILES):
                    if n >= 4:
                        pe.wait_ge(f_sum, 2 * (n - 3))
                    out, c0, c1 = banks[n % 4], n * P, n * P + P
                    pe.matmul(out[:, 0:P], acc[:, 0, c0:c1], w_out[:, 0:P], start=True, stop=False)
                    pe.matmul(out[:, 0:P], acc[:, 1, c0:c1], w_out[:, P:2 * P], start=False, stop=False)
                    pe.matmul(out[:, 0:P], acc[0:64, 2, c0:c1], w_out[0:64, 2 * P:3 * P],
                              start=False, stop=True).then_inc(f_po, 1)

            @block.vector
            def _(dve):
                for row, col in ((0, P), (64, P), (MUL, 2 * P)):
                    view = w_out[row:row + MUL, col:col + P]
                    dve.tensor_scalar(view, view, float(1 / np.sqrt(np.float32(3))), None, ALU.mult).then_inc(f_w, 1)
                for n in range(NODE_TILES):
                    dve.wait_ge(f_po, n + 1)
                    out = banks[n % 4]
                    dve.scalar_tensor_tensor(x1[:, n, 0:MUL], out[:, 0:MUL], scale, x1[:, n, 0:MUL],
                                             ALU.mult, ALU.add).then_inc(f_sum, 1)
                    dve.scalar_tensor_tensor(x1[:, n, MUL:].rearrange("p (u i) -> p u i", i=3),
                                             out[:, MUL:P].rearrange("p (i u) -> p u i", i=3), scale,
                                             x1[:, n, MUL:].rearrange("p (u i) -> p u i", i=3),
                                             ALU.mult, ALU.add).then_inc(f_sum, 1)
                    dve.wait_ge(f_sum, 2 * n + 2)
                    dve.bn_stats(stats[:, n, :], x1[:, n, :]).then_inc(f_st, 1)
                    dve.wait_ge(f_st, n + 1)
                    dve.bn_aggr(moments[:, n, :], stats[:, n, :]).then_inc(f_mom, 1)
                dve.wait_ge(f_sqrt, 1)
                dve.reciprocal(rstd[:], rstd[:]).then_inc(f_rstd, 1)
                dve.wait_ge(f_rstd, 1)
                for n in range(NODE_TILES):
                    dve.tensor_scalar(x1[:, n, :], x1[:, n, :], moments[:, n, 0:1], rstd[:, n:n + 1],
                                      ALU.subtract, ALU.mult).then_inc(f_norm, 1)

            @block.scalar
            def _(act_e):
                act_e.wait_ge(f_mom, NODE_TILES)
                act_e.activation(rstd[:], moments[:, :, 1], ACT.Sqrt, bias=eps[:]).then_inc(f_sqrt, 1)

            @block.sync
            def _(sp):
                full = NODE_TILES - 1
                step = min(12, full)
                for n in range(0, full, step):
                    sp.wait_ge(f_norm, n + step)
                    sp.dma_start(t["out"][n * P:(n + step) * P, :].rearrange("(a p) d -> p a d", p=P),
                                 x1[:, n:n + step, :]).then_inc(f_out, 16)
                sp.wait_ge(f_norm, NODE_TILES)
                sp.dma_start(t["out"][full * P:NODES, :], x1[0:LAST_ROWS, full, :]).then_inc(f_out, 16)
                sp.wait_ge(f_out, 16 * (full // step + 1))


def lay_out(i):
    a = {}
    pad = NODE_COLS - NODES
    a["x_nodes"] = np.pad(i["x"], ((0, pad), (0, 0))).reshape(NODE_TILES, P, DIM).transpose(1, 0, 2)
    a["x_nodes"] = a["x_nodes"].reshape(P, NODE_TILES * DIM)
    a["seq_index"] = (np.pad(i["dst"].reshape(NODES, STEPS), ((0, pad), (0, 0)))
                      .reshape(NODE_TILES, P, STEPS).transpose(1, 0, 2).reshape(P, NODE_TILES * STEPS))
    epad = EDGE_TILES * P - EDGES
    a["dst"] = np.pad(i["dst"], (0, epad), constant_values=FAR).reshape(EDGE_TILES, P).T
    a["src"] = np.pad(i["src"], (0, epad)).reshape(EDGE_TILES, P).T
    a["attr4"] = (np.pad(i["edge_attr_4"], ((0, epad), (0, 0))).reshape(EDGE_TILES, P, 4)
                  .transpose(1, 2, 0).reshape(P, 4 * EDGE_TILES))
    a["attr8"] = (np.pad(i["edge_attr_8"], ((0, epad), (0, 0)))
                  .reshape(EDGE_TILES // SUPER, SUPER // GROUP, 2, HALF, P, 8)
                  .transpose(0, 1, 2, 5, 3, 4).reshape(EDGE_TILES // SUPER, P, HALF * P))
    a["w_ih"] = i["L0_gnn_w_ih"].T
    a["w_hh"] = i["L0_gnn_w_hh"].T
    a["x_t"] = np.pad(i["x"].T, ((0, 0), (0, pad)))
    a["bias2"] = np.broadcast_to(np.concatenate([i["L0_gnn_b_ih"], i["L0_gnn_b_hh"]]), (P, 8 * HID))
    a["w_lin"] = i["L0_gnn_w_lin"].T
    a["b_lin"] = i["L0_gnn_b_lin"].reshape(1, HID)
    up = np.zeros((P, P), np.float32)
    up[0:MUL, 0:MUL] = i["L1_gnn_W_up_s"]
    for k in range(3):
        up[MUL + k::3, MUL * (k + 1):MUL * (k + 2)] = i["L1_gnn_W_up_v"]
    a["w_up"] = up
    a1 = np.zeros((P, GROUP, 2, 64), np.float32)
    a2 = np.zeros((P, P), np.float32)
    for b in range(GROUP):
        for r in range(2):
            a1[16 * b + 8 * r:16 * b + 8 * r + 8, b, r] = i["L1_gnn_A1"]
    for r in range(2):
        a2[64 * r:64 * r + 64, 64 * r:64 * r + 64] = i["L1_gnn_A2"]
    a["a1"] = a1.reshape(P, GROUP * P)
    a["a2"] = a2
    a["a3"] = np.concatenate([i["L1_gnn_A3"], i["L1_gnn_A3"]])
    a["b12"] = np.stack([np.concatenate([i["L1_gnn_b1"]] * 2), np.concatenate([i["L1_gnn_b2"]] * 2)], axis=1)
    ws, wv = i["L1_gnn_W_out_s"], i["L1_gnn_W_out_v"]
    w = np.zeros((3, P, P), np.float32)
    w[0, 0:MUL, 0:MUL] = ws[0:MUL]
    for k in range(3):
        cols = slice(MUL * (k + 1), MUL * (k + 2))
        w[0, cols, cols] = wv[MUL:]
        s3, v1 = (64 * k, 64 * k + MUL) if k < 2 else (MUL, 0)
        w[1 + k // 2, s3:s3 + MUL, 0:MUL] = ws[MUL:]
        w[1 + k // 2, v1:v1 + MUL, cols] = wv[0:MUL]
    a["w_out"] = w.transpose(1, 0, 2).reshape(P, 3 * P)
    a["ident"] = np.eye(P, dtype=np.float32)
    a["base_row"] = np.broadcast_to(BASE.astype(np.float32), (P, EDGE_TILES))
    a["node_iota"] = np.broadcast_to(np.arange(WIN, dtype=np.float32), (P, WIN))
    return {k: np.ascontiguousarray(v) for k, v in a.items()}


def kernel(**inputs):
    import concourse.bacc as bacc
    from concourse.bass_utils import run_bass_kernel_spmd

    arrays = lay_out({k: np.asarray(v) for k, v in inputs.items()})
    nc = bacc.Bacc("TRN2", target_bir_lowering=False, num_devices=1)
    t = {k: nc.dram_tensor(k + "_in", v.shape, mybir.dt.from_np(v.dtype), kind="ExternalInput").ap()
         for k, v in arrays.items()}
    t["table"] = nc.dram_tensor("table", (NODE_COLS, P), F32, kind="Internal").ap()
    t["gates"] = nc.dram_tensor("gates", (NODE_COLS, 4 * HID), F32, kind="Internal").ap()
    t["turned"] = nc.dram_tensor("turned", (3 * P, TURN), F32, kind="Internal").ap()
    t["out"] = nc.dram_tensor("out", (NODES, DIM), F32, kind="ExternalOutput").ap()
    build(nc, t)
    result = run_bass_kernel_spmd(nc, [{k + "_in": v for k, v in arrays.items()}], core_ids=[0])
    return result.results[0]["out"]
```

```python
from contextlib import ExitStack

import numpy as np

import concourse.bass as bass
from concourse import mybir

F32 = mybir.dt.float32
F32R = mybir.dt.float32r
I32 = mybir.dt.int32
BF16 = mybir.dt.bfloat16
ALU = mybir.AluOpType
ACT = mybir.ActivationFunctionType

P = 128
NODES, DIM, HID = 6250, 128, 128
EDGES = 106250
STEPS = EDGES // NODES
MUL = 32
NODE_TILES = -(-NODES // P)
NODE_COLS = NODE_TILES * P
LAST_ROWS = NODES - (NODE_TILES - 1) * P

CHUNK = 512
CHUNKS = [(c, min(CHUNK, NODE_COLS - c)) for c in range(0, NODE_COLS, CHUNK)]
NCH = len(CHUNKS)
FOURS = [range(n, min(n + 4, NODE_TILES)) for n in range(0, NODE_TILES, 4)]
WORK = [(t, c) for t in range(STEPS) for c in range(NCH)]
GATES = (0, 2, 1, 3)

GROUP = 8
HALF = GROUP // 2
SUPER = 64
EDGE_TILES = -(-(-(-EDGES // P)) // SUPER) * SUPER
NGROUP = EDGE_TILES // GROUP
WIN = 80
ROUNDS = -(-NODES // WIN)
TURN = ROUNDS * WIN
FAR = 1 << 24


DVE_FACTORS = 2

PAIR = (4, 6, 7)


def window_bases():
    centre = (np.arange(EDGE_TILES) + 0.5) * P * NODES / EDGES
    base = np.clip(np.rint(centre - WIN / 2), 0, None).astype(int)
    width = max(base[g * GROUP + GROUP - 1] - base[g * GROUP] for g in range(NGROUP)) + WIN
    width += width % 2
    base = np.minimum(base, TURN - width)
    return base, width


BASE, GWIDTH = window_bases()


def build(nc, t):
    ctx = ExitStack()
    with ctx:
        def sb(name, shape, dt=F32, scope=ctx):
            return scope.enter_context(nc.sbuf_tensor(name, shape, dt))

        def ps(name, shape, dt=F32, scope=ctx):
            return scope.enter_context(nc.psum_tensor(name, shape, dt))

        def sem(name):
            return ctx.enter_context(nc.semaphore(name))

        x1 = sb("x1", [P, NODE_TILES, DIM])
        dst = sb("dst", [P, EDGE_TILES])
        rel = sb("rel", [P, EDGE_TILES])
        base_row = sb("base_row", [P, EDGE_TILES])
        src_index = sb("src_index", [P, EDGE_TILES], I32)
        attr = sb("attr", [P, 4, EDGE_TILES])
        node_iota = sb("node_iota", [P, WIN])
        ones = sb("ones", [P, P])
        ident = sb("ident", [P, P])
        eps = sb("eps", [P, 1])
        w_up = sb("w_up", [P, P])
        a1 = sb("a1", [P, GROUP * P])
        a2 = sb("a2", [P, P])
        a3 = sb("a3", [P, P])
        b12 = sb("b12", [P, 2])
        w_out = sb("w_out", [P, 3 * P])
        w_lin = sb("w_lin", [P, P])
        b_lin = sb("b_lin", [P, 1])
        rounds_word = sb("rounds_word", [1, 1], I32)
        zeros = sb("zeros", [P, 3 * GWIDTH], BF16)
        stats = sb("stats", [P, NODE_TILES, 6])
        moments = sb("moments", [P, NODE_TILES, 2])
        rstd = sb("rstd", [P, NODE_TILES])

        acc = sb("acc", [P, 3, max(TURN, NODE_COLS, 12 * CHUNK)])
        banks = [ps(f"bank{i}", [P, 512]) for i in range(8)]

        s_const = sem("s_const")
        s_wait = [sem(f"s_gather{i}") for i in range(4)]

        def flat_view(tile):
            return tile[:].rearrange("p a n -> p (a n)")

        def flat(tile, slot):
            return tile[:, slot].rearrange("p a n -> p (a n)")

        def root(act_e, c, s_mom, s_sqrt):
            tiles = slice(FOURS[c][0], FOURS[c][-1] + 1)
            act_e.wait_ge(s_mom, c + 1)
            act_e.activation(rstd[:, tiles], moments[:, tiles, 1], ACT.Sqrt, bias=eps[:]).then_inc(s_sqrt, 1)

        def normalise(dve, residual, s_sum, s_st, s_mom, s_sqrt, s_rstd, s_norm):
            def moments_of(c):
                dve.wait_ge(s_st, c + 1)
                for n in FOURS[c]:
                    last = dve.bn_aggr(moments[:, n, :], stats[:, n, :])
                last.then_inc(s_mom, 1)

            def invert(c):
                tiles = slice(FOURS[c][0], FOURS[c][-1] + 1)
                dve.wait_ge(s_sqrt, c + 1)
                dve.reciprocal(rstd[:, tiles], rstd[:, tiles]).then_inc(s_rstd, 1)

            def stats_of(c):
                dve.wait_ge(s_sum, c + 1)
                for n in FOURS[c]:
                    last = dve.bn_stats(stats[:, n, :], x1[:, n, :])
                last.then_inc(s_st, 1)

            def scale_rows(c):
                dve.wait_ge(s_rstd, c + 1)
                for n in FOURS[c]:
                    last = dve.tensor_scalar(x1[:, n, :], x1[:, n, :], moments[:, n, 0:1], rstd[:, n:n + 1],
                                             ALU.subtract, ALU.mult)
                last.then_inc(s_norm, 1)

            n = len(FOURS)
            for c in range(n + 2):
                if c < n:
                    residual(c)
                if 1 <= c <= n:
                    moments_of(c - 1)
                if c >= 2:
                    invert(c - 2)
                if c < n:
                    stats_of(c)
                if c >= 2:
                    scale_rows(c - 2)

        with ExitStack() as scope:
            cell = acc[:, 0, :]
            pool_of = acc[:, 1:3, :].rearrange("p a n -> p (a n)")
            rows_cols = 4 * 4 * 4 * HID
            rows = pool_of[:, 0:rows_cols].rearrange("p (s j n) -> p s j n", s=4, j=4)
            act = pool_of[:, rows_cols:rows_cols + 8 * CHUNK].rearrange("p (s g n) -> p s g n", s=2, g=4)
            x_t = cell
            in_rows = rows.rearrange("p s j n -> p (s j) n")
            w_ih = act[:, 0, 0, :]
            inside, inside2 = (act[:, 1].rearrange("p g n -> p (g n)")[:, i:i + EDGE_TILES] for i in (0, 1024))

            seq_index = sb("seq_index", [P, NODE_TILES * STEPS], I32, scope=scope)
            lin_t = sb("lin_t", [P, 2, CHUNK], scope=scope)
            dst_int = flat_view(lin_t).bitcast(I32)[:, 0:EDGE_TILES]
            count = sb("count", [P, 1], scope=scope)
            missed = sb("missed", [1, 1], scope=scope)
            bias2 = sb("bias2", [P, 8], scope=scope)
            w_hi = sb("w_hi", [P, 4 * HID], F32R, scope=scope)
            w_lo = sb("w_lo", [P, 4 * HID], F32R, scope=scope)
            lin_hi = sb("lin_hi", [P, P], F32R, scope=scope)
            lin_lo = sb("lin_lo", [P, P], F32R, scope=scope)
            h_hi = sb("h_hi", [P, NODE_COLS], F32R, scope=scope)
            h_lo = sb("h_lo", [P, NODE_COLS], F32R, scope=scope)
            tanh_c = sb("tanh_c", [P, 2, CHUNK], scope=scope)
            w_hh = tanh_c[:, 0, :]
            up = sb("up", [P, 2, 4, P], scope=scope)

            s_wts, s_idx, s_rest = sem("s_wts"), sem("s_idx"), sem("s_rest")
            s_xt = [sem(f"s_xt{i}") for i in range(5)]
            s_in, s_set, s_hi_x, s_lo_x = (sem(n) for n in ("s_in", "s_set", "s_hi_x", "s_lo_x"))
            s_row = [sem("s_row_vector"), sem("s_row_scalar")]
            s_store = [sem(f"s_store{i}") for i in range(8)]
            s_turned, s_gate, s_act = sem("s_turned"), sem("s_gate"), sem("s_act")
            s_cell, s_tanh, s_hidden = sem("s_cell"), sem("s_tanh"), sem("s_hidden")
            s_ig, s_fc, s_prep, s_count = sem("s_ig"), sem("s_fc"), sem("s_prep"), sem("s_count")
            s_split, s_new, s_hi = sem("s_split"), sem("s_new"), sem("s_hi")

            first = 4
            parts = [np.arange(first), *np.array_split(np.arange(first, NODE_TILES), 4)]

            def part_cols(i):
                return slice(int(parts[i][0]) * P, int(parts[i][-1] + 1) * P)

            def copy_row(engine, n, copy):
                engine.wait_ge(s_in, n + 1)
                if n >= 8:
                    engine.wait_ge(s_store[n % 8], 16 * (n // 8))
                copy(in_rows[:, n % 8, :], banks[n % 8][:]).then_inc(s_row[n % 2], 1)

            with nc.Block() as block:
                @block.sync
                def _(sp):
                    sp.dma_start(w_ih, t["w_ih"]).then_inc(s_wts, 16)
                    for i in range(len(parts)):
                        sp.dma_start(x_t[:, part_cols(i)], t["x_t"][:, part_cols(i)]).then_inc(s_xt[i], 16)
                    sp.dma_start(dst_int, t["dst"]).then_inc(s_const, 16)
                    sp.dma_start(base_row[:], t["base_row"]).then_inc(s_const, 16)
                    for tile, name in ((w_hh, "w_hh"), (w_lin[:], "w_lin"), (ident[:], "ident"),
                                       (seq_index[:], "seq_index"), (bias2[:], "bias2")):
                        sp.dma_start(tile, t[name]).then_inc(s_idx, 16)
                    for n in range(NODE_TILES):
                        sp.wait_ge(s_row[n % 2], n // 2 + 1)
                        sp.dma_start(t["gates"][n * P:(n + 1) * P, :], in_rows[:, n % 8, :]).then_inc(s_store[n % 8], 16)
                    for i in range(8):
                        sp.wait_ge(s_store[i], 16 * len(range(i, NODE_TILES, 8)))

                @block.gpsimd
                def _(pool):
                    pool.memset(ones[:], 1.0)
                    pool.memset(eps[:], 1e-5)
                    pool.memset(zeros[:], 0.0).then_inc(s_set, 1)
                    pool.wait_ge(s_set, 1)

                @block.tensor
                def _(pe):
                    for i, part in enumerate(parts):
                        pe.wait_ge(s_lo_x, i + 2)
                        for n in map(int, part):
                            if n >= 8:
                                pe.wait_ge(s_row[n % 2], n // 2 - 3)
                            nodes = slice(n * P, (n + 1) * P)
                            for x, w in ((h_lo, w_hi), (h_hi, w_lo), (h_hi, w_hi)):
                                last = pe.matmul(banks[n % 8][:], x[:, nodes], w[:], start=(x is h_lo),
                                                 stop=(x is h_hi and w is w_hi))
                            last.then_inc(s_in, 1)
                    pe.wait_ge(s_set, 1)
                    pe.wait_ge(s_row[1], NODE_TILES // 2)
                    pe.wait_ge(s_prep, 5)
                    pe.matmul(banks[7][0:1, 0:1], count[:], ones[:, 0:1], start=True, stop=True).then_inc(s_count, 1)

                @block.scalar
                def _(act_e):
                    def high(i):
                        act_e.wait_ge(s_xt[i], 16)
                        act_e.activation(h_hi[:, part_cols(i)], x_t[:, part_cols(i)], ACT.Copy).then_inc(s_hi_x, 1)

                    high(0)
                    high(1)
                    for i, part in enumerate(parts):
                        for n in map(int, part):
                            if n % 2:
                                copy_row(act_e, n, lambda out, bank: act_e.activation(out, bank, ACT.Copy))
                            if n == part[0] and i + 2 < len(parts):
                                high(i + 2)

                @block.vector
                def _(dve):
                    def low(i):
                        dve.wait_ge(s_hi_x, i + 1)
                        dve.tensor_tensor(h_lo[:, part_cols(i)], x_t[:, part_cols(i)],
                                          h_hi[:, part_cols(i)].bitcast(F32), ALU.subtract).then_inc(s_lo_x, 1)

                    dve.wait_ge(s_wts, 16)
                    dve.tensor_copy(w_hi[:], w_ih).then_inc(s_split, 1)
                    dve.wait_ge(s_split, 1)
                    dve.tensor_tensor(w_lo[:], w_ih, w_hi[:].bitcast(F32), ALU.subtract).then_inc(s_lo_x, 1)
                    low(0)
                    low(1)

                    def as_number():
                        dve.wait_ge(s_const, 32)
                        dve.tensor_copy(dst[:], dst_int).then_inc(s_prep, 1)

                    def relative():
                        dve.wait_ge(s_prep, 1)
                        dve.tensor_tensor(rel[:], dst[:], base_row[:], ALU.subtract).then_inc(s_prep, 1)

                    def not_before():
                        dve.wait_ge(s_prep, 2)
                        dve.tensor_scalar(inside, rel[:], 0.0, None, ALU.is_ge).then_inc(s_prep, 1)

                    def not_after():
                        dve.wait_ge(s_prep, 3)
                        dve.scalar_tensor_tensor(inside2, rel[:], float(WIN), inside, ALU.is_lt,
                                                 ALU.mult).then_inc(s_prep, 1)

                    def per_partition():
                        dve.wait_ge(s_prep, 4)
                        dve.tensor_reduce(count[:], inside2, mybir.AxisListType.X, ALU.add).then_inc(s_prep, 1)

                    def high_weights():
                        dve.wait_ge(s_idx, 16 * 5)
                        dve.tensor_tensor(bias2[:, 0:4], bias2[:, 0:4], bias2[:, 4:8], ALU.add)
                        dve.tensor_copy(lin_hi[:], w_lin[:]).then_inc(s_split, 1)

                    def low_weights():
                        dve.wait_ge(s_split, 2)
                        dve.tensor_tensor(lin_lo[:], w_lin[:], lin_hi[:].bitcast(F32), ALU.subtract)

                    besides = [as_number, relative, not_before, not_after, per_partition, high_weights, low_weights]
                    for i, part in enumerate(parts):
                        for n in map(int, part):
                            if n % 2 == 0:
                                copy_row(dve, n, dve.tensor_copy)
                                if n >= NODE_TILES // 4 and besides:
                                    besides.pop(0)()
                            if n == part[0] + 1 and i + 2 < len(parts):
                                low(i + 2)
                    for step in besides:
                        step()
                    dve.wait_ge(s_count, 1)
                    dve.tensor_scalar(missed[:], banks[7][0:1, 0:1], float(EDGES), float(ROUNDS - 1),
                                      ALU.is_lt, ALU.mult).then_inc(s_prep, 1)
                    dve.wait_ge(s_prep, 6)
                    dve.tensor_scalar(rounds_word[:], missed[:], 1.0, None, ALU.add).then_inc(s_prep, 1)
                    dve.wait_ge(s_prep, 7)

            with nc.Block() as block:
                @block.sync
                def _(sp):
                    small = [(tile[:], t[name]) for tile, name in (
                        (node_iota, "node_iota"), (src_index, "src"), (w_up, "w_up"), (a1, "a1"), (a2, "a2"),
                        (a3, "a3"), (b12, "b12"), (w_out, "w_out"), (b_lin, "b_lin"))]
                    large = [(x1[:, tiles[0]:tiles[-1] + 1, :].rearrange("p a d -> p (a d)"),
                              t["x_nodes"][:, tiles[0] * DIM:(tiles[-1] + 1) * DIM]) for tiles in FOURS]
                    large += [(attr[:, k, :], t["attr4"][:, k * EDGE_TILES:(k + 1) * EDGE_TILES]) for k in range(4)]
                    loads = small + large
                    for i, (tile, source) in enumerate(loads):
                        sp.wait_ge(s_act, 8 * (i + 1))
                        sp.dma_start(tile, source).then_inc(s_rest, 16)
                    sp.wait_ge(s_rest, 16 * len(loads))

                @block.gpsimd
                def _(pool):
                    pool.wait_ge(s_idx, 64)
                    for k, (step, c) in enumerate(WORK):
                        if 4 <= k < NCH + 4:
                            pool.wait_ge(s_gate, 4 * (k - 3))
                        elif k >= 4:
                            pool.wait_ge(s_turned, k - 3 - NCH)
                        c0, width = CHUNKS[c]
                        for j in range(width // P):
                            col = (c0 // P + j) * STEPS + step
                            pool.indirect_dma_start(
                                out=rows[:, k % 4, j, :], out_offset=None, in_=t["gates"],
                                in_offset=bass.IndirectOffsetOnAxis(ap=seq_index[:, col:col + 1], axis=0),
                            ).then_inc(s_wait[k % 4], 16)

                @block.tensor
                def _(pe):
                    landed = [0] * 4
                    pe.wait_ge(s_idx, 64)
                    for k, (step, c) in enumerate(WORK):
                        c0, width = CHUNKS[c]
                        landed[k % 4] += 16 * (width // P)
                        pe.wait_ge(s_wait[k % 4], landed[k % 4])
                        if k >= 2:
                            pe.wait_ge(s_act, 4 * (k - 1))
                        for q, gate in enumerate(GATES):
                            bank, cols = banks[4 * (k % 2) + q], slice(gate * HID, (gate + 1) * HID)
                            for j in range(width // P):
                                last = pe.matmul(bank[:, j * P:(j + 1) * P], rows[:, k % 4, j, cols], ident[:],
                                                 is_transpose=True, start=(j == 0), stop=False,
                                                 skip_group_check=True)
                            if step == 0:
                                last.then_inc(s_gate, 1)
                        if step == 0:
                            continue
                        last.then_inc(s_turned, 1)
                        pe.wait_ge(s_hidden, k - NCH + 1)
                        for q, gate in enumerate(GATES):
                            bank, cols = banks[4 * (k % 2) + q], slice(gate * HID, (gate + 1) * HID)
                            for w, h in ((w_lo, h_hi), (w_hi, h_lo), (w_hi, h_hi)):
                                last = pe.matmul(bank[:, 0:width], w[:, cols], h[:, c0:c0 + width],
                                                 start=False, stop=(w is w_hi and h is h_hi),
                                                 skip_group_check=True)
                            last.then_inc(s_gate, 1)

                @block.scalar
                def _(act_e):
                    def tanh_cell(k):
                        c0, width = CHUNKS[WORK[k][1]]
                        act_e.wait_ge(s_cell, k + 1)
                        if k >= 2:
                            act_e.wait_ge(s_hidden, k - 1)
                        act_e.activation(tanh_c[:, k % 2, 0:width], cell[:, c0:c0 + width],
                                         ACT.Tanh).then_inc(s_tanh, 1)

                    for k, (step, c) in enumerate(WORK):
                        width = CHUNKS[c][1]
                        for q, gate in enumerate(GATES):
                            n = 4 * k + q
                            if q == 0 and k >= 2:
                                act_e.wait_ge(s_cell, k - 1)
                            if q == 3 and k >= 2:
                                act_e.wait_ge(s_hidden, k - 1)
                            act_e.wait_ge(s_gate, n + 1)
                            act_e.activation(act[:, k % 2, gate, 0:width], banks[n % 8][:, 0:width],
                                             ACT.Tanh if gate == 2 else ACT.Sigmoid,
                                             bias=bias2[:, gate:gate + 1]).then_inc(s_act, 1)
                        if k:
                            tanh_cell(k - 1)
                    tanh_cell(len(WORK) - 1)

                @block.vector
                def _(dve):
                    def hidden_product(k):
                        width = CHUNKS[WORK[k][1]][1]
                        dve.wait_ge(s_tanh, k + 1)
                        o = act[:, k % 2, 3, 0:width]
                        dve.tensor_tensor(o, o, tanh_c[:, k % 2, 0:width], ALU.mult).then_inc(s_new, 1)

                    def hidden_hi(k):
                        c0, width = CHUNKS[WORK[k][1]]
                        dve.wait_ge(s_new, k + 1)
                        dve.tensor_copy(h_hi[:, c0:c0 + width], act[:, k % 2, 3, 0:width]).then_inc(s_hi, 1)

                    def hidden_lo(k):
                        c0, width = CHUNKS[WORK[k][1]]
                        dve.wait_ge(s_hi, k + 1)
                        dve.tensor_tensor(h_lo[:, c0:c0 + width], act[:, k % 2, 3, 0:width],
                                          h_hi[:, c0:c0 + width].bitcast(F32), ALU.subtract).then_inc(s_hidden, 1)

                    dve.tensor_copy(w_hi[:], w_hh).then_inc(s_split, 1)
                    dve.wait_ge(s_split, 3)
                    dve.tensor_tensor(w_lo[:], w_hh, w_hi[:].bitcast(F32), ALU.subtract)
                    for k, (step, c) in enumerate(WORK):
                        c0, width = CHUNKS[c]
                        here = cell[:, c0:c0 + width]
                        gates = act[:, k % 2, :, 0:width]
                        n = k - NCH + 1
                        dve.wait_ge(s_act, 4 * k + 2)
                        if step == 0:
                            dve.tensor_tensor(here, gates[:, 0], gates[:, 2], ALU.mult).then_inc(s_cell, 1)
                        else:
                            dve.tensor_tensor(gates[:, 0], gates[:, 0], gates[:, 2], ALU.mult).then_inc(s_ig, 1)
                        if k:
                            hidden_product(k - 1)
                        if step:
                            dve.wait_ge(s_act, 4 * k + 3)
                            dve.tensor_tensor(gates[:, 1], gates[:, 1], here, ALU.mult).then_inc(s_fc, 1)
                        if k:
                            hidden_hi(k - 1)
                        if step:
                            dve.wait_ge(s_ig, n)
                            dve.wait_ge(s_fc, n)
                            dve.tensor_tensor(here, gates[:, 0], gates[:, 1], ALU.add).then_inc(s_cell, 1)
                        if k:
                            hidden_lo(k - 1)
                        dve.wait_ge(s_act, 4 * k + 4)
                    hidden_product(len(WORK) - 1)
                    hidden_hi(len(WORK) - 1)
                    hidden_lo(len(WORK) - 1)

            x1t = tanh_c[:].rearrange("p a (b d) -> p a b d", d=P)
            s_po, s_sum, s_st, s_mom, s_sqrt, s_rstd, s_norm = (sem(n) for n in (
                "s_po", "s_sum", "s_st", "s_mom", "s_sqrt", "s_rstd", "s_norm"))
            s_lin, s_back = sem("s_lin"), sem("s_back")
            s_x1t, s_x1c, s_upp, s_up = (sem(n) for n in ("s_x1t", "s_x1c", "s_upp", "s_up"))
            s_table = [sem(f"s_table{i}") for i in range(2)]
            s_zero = sem("s_zero")
            with nc.Block() as block:
                @block.gpsimd
                def _(pool):
                    pool.memset(acc[:].rearrange("p a b -> p (a b)"), 0.0).then_inc(s_zero, 1)
                    pool.wait_ge(s_zero, 1)

                @block.tensor
                def _(pe):
                    def linear(c):
                        if c >= 2:
                            pe.wait_ge(s_lin, c - 1)
                        width, c0 = P * len(FOURS[c]), P * FOURS[c][0]
                        for w, h in ((lin_lo, h_hi), (lin_hi, h_lo), (lin_hi, h_hi)):
                            last = pe.matmul(banks[c % 2][:, 0:width], w[:], h[:, c0:c0 + width], start=(w is lin_lo),
                                             stop=(w is lin_hi and h is h_hi))
                        last.then_inc(s_po, 1)

                    def turn_back(c):
                        pe.wait_ge(s_lin, c + 1)
                        if c >= 2:
                            pe.wait_ge(s_sum, c - 1)
                        for j in range(len(FOURS[c])):
                            cols = slice(j * P, (j + 1) * P)
                            last = pe.transpose(banks[6 + c % 2][:, cols], lin_t[:, c % 2, cols], ident[:])
                        last.then_inc(s_back, 1)

                    def turn(c):
                        pe.wait_ge(s_norm, c + 1)
                        if c >= 2:
                            pe.wait_ge(s_x1c, c - 1)
                        for j, n in enumerate(FOURS[c]):
                            last = pe.transpose(banks[2 + c % 2][:, j * P:(j + 1) * P], x1[:, n, :], ident[:])
                        last.then_inc(s_x1t, 1)

                    def project(c):
                        pe.wait_ge(s_x1c, c + 1)
                        if c >= 2:
                            pe.wait_ge(s_up, c - 1)
                        for j, n in enumerate(FOURS[c]):
                            last = pe.matmul(banks[4 + c % 2][:, j * P:(j + 1) * P], x1t[:, c % 2, j, :], w_up[:],
                                             start=True, stop=True)
                        last.then_inc(s_upp, 1)

                    for c in range(len(FOURS) + 5):
                        if c < len(FOURS):
                            linear(c)
                        if 1 <= c <= len(FOURS):
                            turn_back(c - 1)
                        if 4 <= c < len(FOURS) + 4:
                            turn(c - 4)
                        if 5 <= c:
                            project(c - 5)

                @block.vector
                def _(dve):
                    def residual(c):
                        tiles = FOURS[c]
                        here = x1[:, tiles[0]:tiles[-1] + 1, :]
                        dve.wait_ge(s_back, c + 1)
                        dve.tensor_tensor(here, here, banks[6 + c % 2][:, 0:P * len(tiles)].rearrange(
                            "p (a d) -> p a d", d=P), ALU.add).then_inc(s_sum, 1)

                    normalise(dve, residual, s_sum, s_st, s_mom, s_sqrt, s_rstd, s_norm)

                @block.scalar
                def _(act_e):
                    def copy_linear(c):
                        width = P * len(FOURS[c])
                        act_e.wait_ge(s_po, c + 1)
                        if c >= 2:
                            act_e.wait_ge(s_back, c - 1)
                        act_e.activation(lin_t[:, c % 2, 0:width], banks[c % 2][:, 0:width], ACT.Identity,
                                         bias=b_lin[:]).then_inc(s_lin, 1)

                    def copy_turned(c):
                        width = P * len(FOURS[c])
                        act_e.wait_ge(s_x1t, c + 1)
                        if c >= 2:
                            act_e.wait_ge(s_upp, c - 1)
                        act_e.activation(flat(x1t, c % 2)[:, 0:width], banks[2 + c % 2][:, 0:width],
                                         ACT.Copy).then_inc(s_x1c, 1)

                    def copy_projected(c):
                        width = P * len(FOURS[c])
                        act_e.wait_ge(s_upp, c + 1)
                        if c >= 2:
                            act_e.wait_ge(s_table[c % 2], 16 * (c // 2))
                        act_e.activation(flat(up, c % 2)[:, 0:width], banks[4 + c % 2][:, 0:width], ACT.Copy,
                                         scale=float(1 / np.sqrt(np.float32(MUL)))).then_inc(s_up, 1)

                    for c in range(len(FOURS) + 5):
                        if c < len(FOURS):
                            copy_linear(c)
                        if 2 <= c < len(FOURS) + 2:
                            root(act_e, c - 2, s_mom, s_sqrt)
                        if 4 <= c < len(FOURS) + 4:
                            copy_turned(c - 4)
                        if 5 <= c:
                            copy_projected(c - 5)

                @block.sync
                def _(sp):
                    for c, tiles in enumerate(FOURS):
                        sp.wait_ge(s_up, c + 1)
                        sp.dma_start(t["table"][tiles[0] * P:(tiles[-1] + 1) * P, :].rearrange("(a p) d -> p a d", p=P),
                                     up[:, c % 2, 0:len(tiles), :]).then_inc(s_table[c % 2], 16)
                    for i in range(2):
                        sp.wait_ge(s_table[i], 16 * len(range(i, len(FOURS), 2)))

        feats = sb("feats", [P, 2, 512])
        h1 = sb("h1", [P, 2, 512])
        h2 = sb("h2", [P, 2, 512])
        sender = sb("sender", [P, 4, HALF, P])
        msg = sb("msg", [P, 2, HALF, 9, MUL])
        select = sb("select", [P, 2, HALF, 4, WIN])
        match = sb("match", [P, 2, HALF, WIN])
        wrap = sb("wrap", [P, EDGE_TILES])

        e_rel, e_turn = sem("e_rel"), sem("e_turn")
        e_feats = [sem("e_feats0"), sem("e_feats1")]
        e_gather = [sem(f"e_gather{i}") for i in range(4)]
        e_p1, e_h1, e_p2, e_h2, e_w = (sem(n) for n in ("e_p1", "e_h1", "e_p2", "e_h2", "e_w"))
        e_match, e_sel, e_sel2, e_msg, e_half, e_group, e_acc = (
            sem(n) for n in ("e_match", "e_sel", "e_sel2", "e_msg", "e_half", "e_group", "e_acc"))
        e_sems = [e_rel, e_turn, *e_feats, *e_gather, e_p1, e_h1, e_p2, e_h2, e_w,
                  e_match, e_sel, e_sel2, e_msg, e_half, e_group, e_acc]
        p1_bank, p2_bank = banks[0], banks[1]
        weight_bank, acc_bank = banks[2:5], banks[5:7]
        NHALF = 2 * NGROUP

        rounds = nc.values_load(rounds_word[0:1, 0:1], min_val=1, max_val=ROUNDS)

        with nc.Fori(0, rounds):
            with nc.Block() as block:
                @block.sync
                def _(sp):
                    for s in range(EDGE_TILES // SUPER):
                        if s >= 2:
                            sp.wait_ge(e_p1, GROUP * (s - 1))
                        sp.dma_start(feats[:, s % 2, :], t["attr8"][s]).then_inc(e_feats[s % 2], 16)

                @block.gpsimd
                def _(pool):
                    for hg in range(NHALF):
                        if hg >= 4:
                            pool.wait_ge(e_msg, hg - 3)
                        for j in range(HALF):
                            tile = hg * HALF + j
                            pool.indirect_dma_start(
                                out=sender[:, hg % 4, j, :], out_offset=None, in_=t["table"],
                                in_offset=bass.IndirectOffsetOnAxis(ap=src_index[:, tile:tile + 1], axis=0),
                            ).then_inc(e_gather[hg % 4], 16)

                @block.tensor
                def _(pe):
                    def mlp1(g):
                        if g >= NGROUP:
                            return
                        s, b = divmod(g, SUPER // GROUP)
                        if b == 0:
                            pe.wait_ge(e_feats[s % 2], 16 * (s // 2 + 1))
                        if g:
                            pe.wait_ge(e_h1, g)
                        pe.matmul(p1_bank[:], a1[:, b * P:(b + 1) * P], feats[:, s % 2, :],
                                  start=True, stop=True).then_inc(e_p1, 1)

                    def mlp2(g):
                        if g >= NGROUP:
                            return
                        pe.wait_ge(e_h1, g + 1)
                        if g:
                            pe.wait_ge(e_h2, g)
                        pe.matmul(p2_bank[:], a2[:], h1[:, g % 2, :], start=True, stop=True).then_inc(e_p2, 1)

                    def mlp3(hg):
                        if hg >= NHALF:
                            return
                        g, half = divmod(hg, 2)
                        if half == 0:
                            pe.wait_ge(e_h2, g + 1)
                        if hg >= 3:
                            pe.wait_ge(e_msg, hg - 2)
                        for j in range(HALF):
                            channels = slice(64 * half, 64 * half + 64)
                            last = pe.matmul(weight_bank[hg % 3][:, j * P:(j + 1) * P],
                                             h2[channels, g % 2, j * P:(j + 1) * P],
                                             a3[channels, :], start=True, stop=True)
                        last.then_inc(e_w, 1)

                    def sum_receivers(hg):
                        g, half = divmod(hg, 2)
                        bank = acc_bank[g % 2]
                        if half == 0:
                            if g >= 2:
                                pe.wait_ge(e_acc, g - 1)
                            pe.matmul(bank[:, 0:3 * GWIDTH], zeros[:, 0:P], zeros[:], start=True, stop=False,
                                      skip_group_check=True)
                        pe.wait_ge(e_sel, hg + 1)
                        pe.wait_ge(e_sel2, hg + 1)
                        pe.wait_ge(e_msg, hg + 1)
                        for j in range(HALF):
                            tile = hg * HALF + j
                            off = int(BASE[tile] - BASE[g * GROUP])
                            m = msg[:, hg % 2, j]
                            sel = select[:, hg % 2, j]
                            pe.matmul(bank[:, off:off + WIN], m[:, 0:4, :], sel[:, 0, :],
                                      start=False, stop=False, skip_group_check=True)
                            for i in range(3):
                                lo = GWIDTH * (1 + i // 2) + off
                                last = pe.matmul(bank[64 * (i % 2):64 * (i % 2) + 64, lo:lo + WIN],
                                                 m[:, PAIR[i]:PAIR[i] + 2, :], sel[:, i + 1, :],
                                                 start=False, stop=(half == 1 and j == HALF - 1 and i == 2),
                                                 skip_group_check=True)
                        last.then_inc(e_half, 1)

                    for g in range(3):
                        mlp1(g)
                        if g >= 1:
                            mlp2(g - 1)
                    for hg in range(2):
                        mlp3(hg)
                    for g in range(NGROUP):
                        mlp1(g + 3)
                        mlp2(g + 2)
                        for half in range(2):
                            mlp3(2 * g + 2 + half)
                            sum_receivers(2 * g + half)

                @block.scalar
                def _(act_e):
                    def silu1(g):
                        if g >= NGROUP:
                            return
                        act_e.wait_ge(e_p1, g + 1)
                        if g >= 2:
                            act_e.wait_ge(e_p2, g - 1)
                        act_e.activation(h1[:, g % 2, :], p1_bank[:], ACT.Silu, bias=b12[:, 0:1]).then_inc(e_h1, 1)

                    def silu2(g):
                        if g >= NGROUP:
                            return
                        act_e.wait_ge(e_p2, g + 1)
                        if g >= 2:
                            act_e.wait_ge(e_w, 2 * (g - 1))
                        act_e.activation(h2[:, g % 2, :], p2_bank[:], ACT.Silu, bias=b12[:, 1:2]).then_inc(e_h2, 1)

                    def selections(hg):
                        act_e.wait_ge(e_match, hg + 1)
                        if hg >= 2:
                            act_e.wait_ge(e_half, hg - 1)
                        for j in range(HALF):
                            tile = hg * HALF + j
                            for k in range(DVE_FACTORS, 4):
                                last = act_e.activation(select[:, hg % 2, j, k, :], match[:, hg % 2, j], ACT.Copy,
                                                        scale=attr[:, k, tile:tile + 1])
                        last.then_inc(e_sel2, 1)

                    for g in range(2):
                        silu1(g)
                    silu2(0)
                    silu1(2)
                    silu2(1)
                    for g in range(NGROUP):
                        selections(2 * g)
                        silu1(g + 3)
                        selections(2 * g + 1)
                        silu2(g + 2)

                @block.vector
                def _(dve):
                    dve.tensor_tensor(rel[:], dst[:], base_row[:], ALU.subtract).then_inc(e_rel, 1)
                    dve.wait_ge(e_rel, 1)

                    def selections(hg):
                        if hg >= NHALF:
                            return
                        if hg >= 2:
                            dve.wait_ge(e_half, hg - 1)
                            dve.wait_ge(e_sel2, hg - 1)
                        tiles = slice(hg * HALF, hg * HALF + HALF)
                        full = [P, HALF, WIN]
                        dve.tensor_tensor(match[:, hg % 2], node_iota[:].rearrange("p (a n) -> p a n", a=1).to_broadcast(full),
                                          rel[:, tiles].rearrange("p (j n) -> p j n", n=1).to_broadcast(full),
                                          ALU.is_equal).then_inc(e_match, 1)
                        dve.wait_ge(e_match, hg + 1)
                        for k in range(DVE_FACTORS):
                            last = dve.tensor_tensor(
                                select[:, hg % 2, :, k, :], match[:, hg % 2],
                                attr[:, k, tiles].rearrange("p (j n) -> p j n", n=1).to_broadcast(full), ALU.mult)
                        last.then_inc(e_sel, 1)

                    def messages(hg):
                        dve.wait_ge(e_w, hg + 1)
                        dve.wait_ge(e_gather[hg % 4], 16 * HALF * (hg // 4 + 1))
                        m = msg[:, hg % 2]
                        w = weight_bank[hg % 3][:].rearrange("p (j v u) -> p j v u", j=HALF, v=4)
                        row = sender[:, hg % 4].rearrange("p j (k u) -> p j k u", k=4)
                        dve.tensor_tensor(m[:, :, 0, :], row[:, :, 0, :], w[:, :, 0, :], ALU.mult)
                        dve.tensor_tensor(m[:, :, 5:8:2, :], row[:, :, 0:1, :].to_broadcast([P, HALF, 2, MUL]),
                                          w[:, :, 1:2, :].to_broadcast([P, HALF, 2, MUL]), ALU.mult)
                        dve.tensor_tensor(m[:, :, 1:4, :], row[:, :, 1:4, :],
                                          w[:, :, 2:3, :].to_broadcast([P, HALF, 3, MUL]), ALU.mult)
                        last = dve.tensor_tensor(m[:, :, 4:9:2, :], row[:, :, 1:4, :],
                                                 w[:, :, 3:4, :].to_broadcast([P, HALF, 3, MUL]), ALU.mult)
                        last.then_inc(e_msg, 1)

                    def add_group(g):
                        dve.wait_ge(e_half, 2 * g + 2)
                        if g:
                            dve.wait_ge(e_group, g)
                        at = int(BASE[g * GROUP])
                        dve.tensor_tensor(acc[:, 0:2, at:at + GWIDTH], acc[:, 0:2, at:at + GWIDTH],
                                          acc_bank[g % 2][:, 0:2 * GWIDTH].rearrange("p (a n) -> p a n", a=2),
                                          ALU.add).then_inc(e_group, 1)
                        dve.tensor_tensor(acc[0:64, 2, at:at + GWIDTH], acc[0:64, 2, at:at + GWIDTH],
                                          acc_bank[g % 2][0:64, 2 * GWIDTH:3 * GWIDTH], ALU.add).then_inc(e_acc, 1)
                        dve.wait_ge(e_acc, g + 1)

                    selections(0)
                    for hg in range(NHALF):
                        messages(hg)
                        selections(hg + 1)
                        if hg % 2 == 0 and hg:
                            add_group(hg // 2 - 1)
                    add_group(NGROUP - 1)
                    dve.tensor_scalar(dst[:], dst[:], -float(WIN), None, ALU.add).then_inc(e_rel, 1)
                    dve.wait_ge(e_rel, 2)
                    dve.tensor_scalar(wrap[:], dst[:], 0.0, float(TURN), ALU.is_lt, ALU.mult).then_inc(e_rel, 1)
                    dve.wait_ge(e_rel, 3)
                    dve.tensor_tensor(dst[:], dst[:], wrap[:], ALU.add).then_inc(e_rel, 1)
                    dve.wait_ge(e_rel, 4)

            with nc.Block() as block:
                @block.sync
                def _(sp):
                    turned = t["turned"].rearrange("(p a) n -> p a n", p=P)
                    with sp.If(rounds > 1):
                        sp.dma_start(turned, acc[:, :, 0:TURN]).then_inc(e_turn, 16)
                        sp.wait_ge(e_turn, 16)
                        sp.dma_start(acc[:, :, 0:TURN - WIN], turned[:, :, WIN:TURN]).then_inc(e_turn, 16)
                        sp.dma_start(acc[:, :, TURN - WIN:TURN], turned[:, :, 0:WIN]).then_inc(e_turn, 16)
                        sp.wait_ge(e_turn, 48)
            with nc.Block() as block:
                @block.gpsimd
                def _(pool):
                    with pool.If(rounds > 1):
                        pool.dma_reset(range(e_gather[0].num, e_gather[3].num + 1))
                        for s in e_sems:
                            pool.sem_clear(s)

        f_po, f_sum, f_mom, f_sqrt, f_rstd, f_norm, f_st, f_out, f_w = (sem(n) for n in (
            "f_po", "f_sum", "f_mom", "f_sqrt", "f_rstd", "f_norm", "f_st", "f_out", "f_w"))
        scale = float(1 / np.sqrt(np.float32(2 * MUL))) / 10.0
        with nc.Block() as block:
            @block.tensor
            def _(pe):
                pe.wait_ge(f_w, 3)
                for c, tiles in enumerate(FOURS):
                    if c >= 4:
                        pe.wait_ge(f_sum, c - 3)
                    for j, n in enumerate(tiles):
                        out, nodes = banks[c % 4][:, j * P:(j + 1) * P], slice(n * P, (n + 1) * P)
                        pe.matmul(out, acc[:, 0, nodes], w_out[:, 0:P], start=True, stop=False)
                        pe.matmul(out, acc[:, 1, nodes], w_out[:, P:2 * P], start=False, stop=False)
                        last = pe.matmul(out, acc[0:64, 2, nodes], w_out[0:64, 2 * P:3 * P], start=False, stop=True)
                    last.then_inc(f_po, 1)

            @block.vector
            def _(dve):
                for row, col in ((0, P), (64, P), (MUL, 2 * P)):
                    view = w_out[row:row + MUL, col:col + P]
                    dve.tensor_scalar(view, view, float(1 / np.sqrt(np.float32(3))), None, ALU.mult).then_inc(f_w, 1)

                def residual(c):
                    tiles = FOURS[c]
                    here = x1[:, tiles[0]:tiles[-1] + 1, :].rearrange("p a d -> p (a d)")
                    dve.wait_ge(f_po, c + 1)
                    dve.scalar_tensor_tensor(here, banks[c % 4][:, 0:P * len(tiles)], scale, here,
                                             ALU.mult, ALU.add).then_inc(f_sum, 1)

                normalise(dve, residual, f_sum, f_st, f_mom, f_sqrt, f_rstd, f_norm)

            @block.scalar
            def _(act_e):
                for c in range(len(FOURS)):
                    root(act_e, c, f_mom, f_sqrt)

            @block.sync
            def _(sp):
                for c, tiles in enumerate(FOURS):
                    sp.wait_ge(f_norm, c + 1)
                    whole = [n for n in tiles if n < NODE_TILES - 1]
                    if whole:
                        sp.dma_start(t["out"][whole[0] * P:(whole[-1] + 1) * P, :].rearrange("(a p) d -> p a d", p=P),
                                     x1[:, whole[0]:whole[-1] + 1, :]).then_inc(f_out, 16)
                full = NODE_TILES - 1
                sp.dma_start(t["out"][full * P:NODES, :], x1[0:LAST_ROWS, full, :]).then_inc(f_out, 16)
                sp.wait_ge(f_out, 16 * (1 + -(-full // 4)))


def lay_out(i):
    a = {}
    pad = NODE_COLS - NODES
    a["x_nodes"] = np.pad(i["x"], ((0, pad), (0, 0))).reshape(NODE_TILES, P, DIM).transpose(1, 0, 2)
    a["x_nodes"] = a["x_nodes"].reshape(P, NODE_TILES * DIM)
    a["seq_index"] = (np.pad(i["dst"].reshape(NODES, STEPS), ((0, pad), (0, 0)))
                      .reshape(NODE_TILES, P, STEPS).transpose(1, 0, 2).reshape(P, NODE_TILES * STEPS))
    epad = EDGE_TILES * P - EDGES
    a["dst"] = np.pad(i["dst"], (0, epad), constant_values=FAR).reshape(EDGE_TILES, P).T
    a["src"] = np.pad(i["src"], (0, epad)).reshape(EDGE_TILES, P).T
    a["attr4"] = (np.pad(i["edge_attr_4"], ((0, epad), (0, 0))).reshape(EDGE_TILES, P, 4)
                  .transpose(1, 2, 0).reshape(P, 4 * EDGE_TILES))
    a["attr8"] = (np.pad(i["edge_attr_8"], ((0, epad), (0, 0)))
                  .reshape(EDGE_TILES // SUPER, SUPER // GROUP, 2, HALF, P, 8)
                  .transpose(0, 1, 2, 5, 3, 4).reshape(EDGE_TILES // SUPER, P, HALF * P))
    a["w_ih"] = i["L0_gnn_w_ih"].T
    a["w_hh"] = i["L0_gnn_w_hh"].T
    a["x_t"] = np.pad(i["x"].T, ((0, 0), (0, pad)))
    a["bias2"] = np.concatenate([i["L0_gnn_b_ih"].reshape(4, HID), i["L0_gnn_b_hh"].reshape(4, HID)]).T
    a["w_lin"] = i["L0_gnn_w_lin"].T
    a["b_lin"] = i["L0_gnn_b_lin"].reshape(HID, 1)
    up = np.zeros((P, P), np.float32)
    up[0:MUL, 0:MUL] = i["L1_gnn_W_up_s"]
    for k in range(3):
        up[MUL + k::3, MUL * (k + 1):MUL * (k + 2)] = i["L1_gnn_W_up_v"]
    a["w_up"] = up
    a1 = np.zeros((P, GROUP, 2, 64), np.float32)
    a2 = np.zeros((P, P), np.float32)
    for b in range(GROUP):
        for r in range(2):
            a1[16 * b + 8 * r:16 * b + 8 * r + 8, b, r] = i["L1_gnn_A1"]
    for r in range(2):
        a2[64 * r:64 * r + 64, 64 * r:64 * r + 64] = i["L1_gnn_A2"]
    a["a1"] = a1.reshape(P, GROUP * P)
    a["a2"] = a2
    a["a3"] = np.concatenate([i["L1_gnn_A3"], i["L1_gnn_A3"]])
    a["b12"] = np.stack([np.concatenate([i["L1_gnn_b1"]] * 2), np.concatenate([i["L1_gnn_b2"]] * 2)], axis=1)
    ws, wv = i["L1_gnn_W_out_s"], i["L1_gnn_W_out_v"]
    w = np.zeros((3, P, P), np.float32)
    w[0, 0:MUL, 0:MUL] = ws[0:MUL]
    for k in range(3):
        cols = slice(MUL + k, P, 3)
        w[0, MUL * (k + 1):MUL * (k + 2), cols] = wv[MUL:]
        s3, v1 = (64 * k, 64 * k + MUL) if k < 2 else (MUL, 0)
        w[1 + k // 2, s3:s3 + MUL, 0:MUL] = ws[MUL:]
        w[1 + k // 2, v1:v1 + MUL, cols] = wv[0:MUL]
    a["w_out"] = w.transpose(1, 0, 2).reshape(P, 3 * P)
    a["ident"] = np.eye(P, dtype=np.float32)
    a["base_row"] = np.broadcast_to(BASE.astype(np.float32), (P, EDGE_TILES))
    a["node_iota"] = np.broadcast_to(np.arange(WIN, dtype=np.float32), (P, WIN))
    return {k: np.ascontiguousarray(v) for k, v in a.items()}


def kernel(**inputs):
    import concourse.bacc as bacc
    from concourse.bass_utils import run_bass_kernel_spmd

    arrays = lay_out({k: np.asarray(v) for k, v in inputs.items()})
    nc = bacc.Bacc("TRN2", target_bir_lowering=False, num_devices=1)
    t = {k: nc.dram_tensor(k + "_in", v.shape, mybir.dt.from_np(v.dtype), kind="ExternalInput").ap()
         for k, v in arrays.items()}
    t["table"] = nc.dram_tensor("table", (NODE_COLS, P), F32, kind="Internal").ap()
    t["gates"] = nc.dram_tensor("gates", (NODE_COLS, 4 * HID), F32, kind="Internal").ap()
    t["turned"] = nc.dram_tensor("turned", (3 * P, TURN), F32, kind="Internal").ap()
    t["out"] = nc.dram_tensor("out", (NODES, DIM), F32, kind="ExternalOutput").ap()
    build(nc, t)
    result = run_bass_kernel_spmd(nc, [{k + "_in": v for k, v in arrays.items()}], core_ids=[0])
    return result.results[0]["out"]
```
